# Optimizing a Trainium2 kernel written in Bass

```python
import numpy as np
import jax
import jax.numpy as jnp

def _softmax(x, axis=-1):
    return jax.nn.softmax(x, axis=axis)

def _gelu(x):
    return jax.nn.gelu(x, approximate=True)

def _silu(x):
    return jax.nn.silu(x)

def _sigmoid(x):
    return jax.nn.sigmoid(x)

def _layernorm(x, axis=-1, eps=1e-05):
    m = jnp.mean(x, axis=axis, keepdims=True)
    v = jnp.var(x, axis=axis, keepdims=True)
    return (x - m) / jnp.sqrt(v + eps)

def _scatter_add(tgt, idx, src, axis=0):
    return tgt.at[idx].add(src)

def _segment_sum(src, seg, n):
    return jax.ops.segment_sum(src, seg, n)
kernel_name = 'mk_pixart_seq_d1_seqx_r4_846424'

def setup_inputs(seed: int=0):
    np.random.seed(seed)
    _w = jnp.asarray

    def _rec_inputs():
        import jax
        import jax.numpy as jnp
        _rk = jax.random.key(seed)
        x = -0.0002928 + 1 * jax.random.normal(jax.random.fold_in(_rk, 1), (32, 256, 256), jnp.float32)
        _lenS = 256 - jax.random.randint(jax.random.fold_in(_rk, 7), (32,), 0, max(1, 256 // 4) + 1, jnp.int32)
        _lenS2 = 256 - jax.random.randint(jax.random.fold_in(_rk, 8), (32,), 0, max(1, 256 // 4) + 1, jnp.int32)
        cond_1024 = 0.0061147 + 1.02565 * jax.random.normal(jax.random.fold_in(_rk, 11), (32, 256), jnp.float32)
        _ctx_1024P = jax.random.normal(jax.random.fold_in(_rk, 12), (32, 16, 256), jnp.float32)
        _ctx_1024c = jax.random.dirichlet(jax.random.fold_in(_rk, 512), 0.3 * jnp.ones((16,), jnp.float32), (32, 256))
        _ctx_1024t = jnp.einsum('bsk,bkd->bsd', _ctx_1024c, _ctx_1024P)
        _ctx_1024t = _ctx_1024t * jax.lax.rsqrt(jnp.mean(jnp.square(_ctx_1024t)) + 1e-12) * 0.953939
        ctx_1024 = -0.00265004 + 0.998804 * (_ctx_1024t + 0.3 * jax.random.normal(jax.random.fold_in(_rk, 612), (32, 256, 256), jnp.float32))
        return (x, cond_1024, ctx_1024)
    x, cond_1024, ctx_1024 = _rec_inputs()

    def _L0_xcond_setup():
        import jax, jax.numpy as jnp
        import numpy as np
        LN_EPS = 1e-06

        def _ln(x):
            mu = jnp.mean(x, axis=-1, keepdims=True)
            var = jnp.var(x, axis=-1, keepdims=True)
            return (x - mu) * jax.lax.rsqrt(var + LN_EPS)
        key = jax.random.key(seed)
        H, NH = (256, 16)
        B, N, S = (4, 256, 77)
        MLP = int(H * 4.0)
        ks = jax.random.split(key, 20)
        s = 1.0 / np.sqrt(H)
        return {'x': jax.random.normal(ks[0], (B, N, H), jnp.float32), 'c': jax.random.normal(ks[1], (B, H), jnp.float32), 'context': jax.random.normal(ks[2], (B, S, H), jnp.float32), 'W_mod': jax.random.normal(ks[3], (H, 6 * H), jnp.float32) * s, 'b_mod': jnp.zeros((6 * H,), jnp.float32), 'W_qkv': jax.random.normal(ks[4], (H, 3 * H), jnp.float32) * s, 'b_qkv': jnp.zeros((3 * H,), jnp.float32), 'W_proj': jax.random.normal(ks[5], (H, H), jnp.float32) * s, 'b_proj': jnp.zeros((H,), jnp.float32), 'W_qc': jax.random.normal(ks[6], (H, H), jnp.float32) * s, 'b_qc': jnp.zeros((H,), jnp.float32), 'W_kvc': jax.random.normal(ks[7], (H, 2 * H), jnp.float32) * s, 'b_kvc': jnp.zeros((2 * H,), jnp.float32), 'W_cproj': jax.random.normal(ks[8], (H, H), jnp.float32) * s, 'b_cproj': jnp.zeros((H,), jnp.float32), 'W_mlp1': jax.random.normal(ks[9], (H, MLP), jnp.float32) * s, 'b_mlp1': jnp.zeros((MLP,), jnp.float32), 'W_mlp2': jax.random.normal(ks[10], (MLP, H), jnp.float32) * (1.0 / np.sqrt(MLP)), 'b_mlp2': jnp.zeros((H,), jnp.float32)}
    _L0_xcond_all = _L0_xcond_setup()
    _L0_xcond_in = {k: v for k, v in _L0_xcond_all.items() if k in ('W_mod', 'b_mod', 'W_qkv', 'b_qkv', 'W_proj', 'b_proj', 'W_qc', 'b_qc', 'W_kvc', 'b_kvc', 'W_cproj', 'b_cproj', 'W_mlp1', 'b_mlp1', 'W_mlp2', 'b_mlp2')}
    del _L0_xcond_all
    return {'x': x, 'cond_1024': cond_1024, 'ctx_1024': ctx_1024, 'L0_xcond_W_mod': _L0_xcond_in['W_mod'], 'L0_xcond_b_mod': _L0_xcond_in['b_mod'], 'L0_xcond_W_qkv': _L0_xcond_in['W_qkv'], 'L0_xcond_b_qkv': _L0_xcond_in['b_qkv'], 'L0_xcond_W_proj': _L0_xcond_in['W_proj'], 'L0_xcond_b_proj': _L0_xcond_in['b_proj'], 'L0_xcond_W_qc': _L0_xcond_in['W_qc'], 'L0_xcond_b_qc': _L0_xcond_in['b_qc'], 'L0_xcond_W_kvc': _L0_xcond_in['W_kvc'], 'L0_xcond_b_kvc': _L0_xcond_in['b_kvc'], 'L0_xcond_W_cproj': _L0_xcond_in['W_cproj'], 'L0_xcond_b_cproj': _L0_xcond_in['b_cproj'], 'L0_xcond_W_mlp1': _L0_xcond_in['W_mlp1'], 'L0_xcond_b_mlp1': _L0_xcond_in['b_mlp1'], 'L0_xcond_W_mlp2': _L0_xcond_in['W_mlp2'], 'L0_xcond_b_mlp2': _L0_xcond_in['b_mlp2']}

def reference(x, cond_1024, ctx_1024, L0_xcond_W_mod, L0_xcond_b_mod, L0_xcond_W_qkv, L0_xcond_b_qkv, L0_xcond_W_proj, L0_xcond_b_proj, L0_xcond_W_qc, L0_xcond_b_qc, L0_xcond_W_kvc, L0_xcond_b_kvc, L0_xcond_W_cproj, L0_xcond_b_cproj, L0_xcond_W_mlp1, L0_xcond_b_mlp1, L0_xcond_W_mlp2, L0_xcond_b_mlp2):
    import jax
    import jax.numpy as jnp

    def _L0_xcond_ref(x, c, context, W_mod, b_mod, W_qkv, b_qkv, W_proj, b_proj, W_qc, b_qc, W_kvc, b_kvc, W_cproj, b_cproj, W_mlp1, b_mlp1, W_mlp2, b_mlp2):
        import jax, jax.numpy as jnp
        import numpy as np
        LN_EPS = 1e-06

        def _ln(x):
            mu = jnp.mean(x, axis=-1, keepdims=True)
            var = jnp.var(x, axis=-1, keepdims=True)
            return (x - mu) * jax.lax.rsqrt(var + LN_EPS)
        B, N, H = x.shape
        NH = 16
        hd = H // NH
        scale = hd ** (-0.5)
        c_proj = jax.nn.silu(c) @ W_mod + b_mod
        shift_a, scale_a, gate_a, shift_m, scale_m, gate_m = jnp.split(c_proj, 6, axis=-1)

        def modulate(t, shift, sc):
            return t * (1 + sc[:, None]) + shift[:, None]
        x_norm = modulate(_ln(x), shift_a, scale_a)
        qkv = x_norm @ W_qkv + b_qkv
        q, k, v = jnp.split(qkv, 3, axis=-1)
        q = q.reshape(B, N, NH, hd).transpose(0, 2, 1, 3)
        k = k.reshape(B, N, NH, hd).transpose(0, 2, 1, 3)
        v = v.reshape(B, N, NH, hd).transpose(0, 2, 1, 3)
        attn_w = jax.nn.softmax(jnp.einsum('bhqd,bhkd->bhqk', q, k) * scale, axis=-1)
        attn_out = jnp.einsum('bhqk,bhkd->bhqd', attn_w, v)
        attn_out = attn_out.transpose(0, 2, 1, 3).reshape(B, N, H)
        attn_out = attn_out @ W_proj + b_proj
        x = x + gate_a[:, None] * attn_out
        S = context.shape[1]
        q_c = _ln(x) @ W_qc + b_qc
        kv_c = _ln(context) @ W_kvc + b_kvc
        k_c, v_c = jnp.split(kv_c, 2, axis=-1)
        q_c = q_c.reshape(B, N, NH, hd).transpose(0, 2, 1, 3)
        k_c = k_c.reshape(B, S, NH, hd).transpose(0, 2, 1, 3)
        v_c = v_c.reshape(B, S, NH, hd).transpose(0, 2, 1, 3)
        c_attn_w = jax.nn.softmax(jnp.einsum('bhqd,bhsd->bhqs', q_c, k_c) * scale, axis=-1)
        c_attn_out = jnp.einsum('bhqs,bhsd->bhqd', c_attn_w, v_c)
        c_attn_out = c_attn_out.transpose(0, 2, 1, 3).reshape(B, N, H)
        c_attn_out = c_attn_out @ W_cproj + b_cproj
        x = x + c_attn_out
        x_norm2 = modulate(_ln(x), shift_m, scale_m)
        h = jax.nn.gelu(x_norm2 @ W_mlp1 + b_mlp1)
        h = h @ W_mlp2 + b_mlp2
        x = x + gate_m[:, None] * h
        return x
    x = _L0_xcond_ref(x, cond_1024, ctx_1024, L0_xcond_W_mod, L0_xcond_b_mod, L0_xcond_W_qkv, L0_xcond_b_qkv, L0_xcond_W_proj, L0_xcond_b_proj, L0_xcond_W_qc, L0_xcond_b_qc, L0_xcond_W_kvc, L0_xcond_b_kvc, L0_xcond_W_cproj, L0_xcond_b_cproj, L0_xcond_W_mlp1, L0_xcond_b_mlp1, L0_xcond_W_mlp2, L0_xcond_b_mlp2)
    return x

_drawn_inputs = setup_inputs


def setup_inputs(seed=0):
    import zlib

    import numpy as np

    out = dict(_drawn_inputs(seed))
    spreads = {'L0_xcond_b_mod': (0.0, 0.1),
     'L0_xcond_b_qkv': (0.0, 0.1),
     'L0_xcond_b_proj': (0.0, 0.1),
     'L0_xcond_b_qc': (0.0, 0.578),
     'L0_xcond_b_kvc': (0.0, 0.1),
     'L0_xcond_b_cproj': (0.0, 0.1),
     'L0_xcond_b_mlp1': (0.0, 0.1),
     'L0_xcond_b_mlp2': (0.0, 0.1)}
    factors = {}
    for name, (base, spread) in spreads.items():
        noise = np.random.default_rng([zlib.crc32(name.encode()), seed]).standard_normal(out[name].shape)
        drawn = base * np.exp(spread * noise) if base else spread * noise
        out[name] = jnp.asarray(drawn.astype(out[name].dtype))
    for name, factor in factors.items():
        out[name] = (out[name] * factor).astype(out[name].dtype)
    return out
```

```python
from contextlib import ExitStack

import concourse.bass as bass
from concourse import mybir

F32 = mybir.dt.float32
F16 = mybir.dt.float16
ALU = mybir.AluOpType
ACT = mybir.ActivationFunctionType
AX_X = mybir.AxisListType.X

P = 128
LN_EPS = 1e-6
TILES = 16
SHIFT_UNIT = 64.0

PLAN = {
    "load_x": (-1, 0, 7), "cols_a": (-1, 0, 8), "ln1": (-1, 0, 14), "t1": (-1, 1, 3),
    "q": (-1, 1, 7), "spill_q": (-1, 1, 9), "stack_q": (-1, 1, 11),
    "k": (-1, 1, 9), "spill_k": (-1, 1, 11), "stack_k": (-1, 1, 13), "v": (-1, 1, 12),
    "split_self": (0, 1, 0), "m_self": (0, 1, 1), "m_copy_self": (0, 1, 2),
    "o_store0_self": (0, 1, 15), "o_store1_self": (1, 0, 8), "o_gather_self": (1, 0, 10),
    "o_recip_self": (1, 0, 12), "r_out_self": (1, 0, 13), "r_back_self": (1, 0, 15),
    "o_norm_self": (1, 1, 0), "o_hi_self": (1, 1, 2),
    "rows_a": (1, 0, 1), "xr": (1, 0, 5), "proj": (1, 1, 4), "ln2": (1, 1, 6),
    "t2": (1, 1, 15), "qc": (2, 0, 3), "spill_qc": (2, 0, 5), "stack_qc": (2, 0, 7),
    "load_c": (1, 1, 5), "lnc": (1, 1, 10), "tc": (2, 0, 5), "kc": (2, 0, 7), "vc": (2, 0, 14),
    "spill_kc": (2, 0, 9), "stack_kc": (2, 0, 11), "xc": (2, 1, 8),
    "split_cross": (3, 0, 0), "m_cross": (3, 0, 1), "m_copy_cross": (3, 0, 2),
    "o_store0_cross": (3, 0, 15), "o_store1_cross": (3, 1, 8), "o_gather_cross": (3, 1, 10),
    "o_recip_cross": (3, 1, 12), "r_out_cross": (3, 1, 13), "r_back_cross": (3, 1, 15),
    "o_norm_cross": (4, 0, 0), "o_hi_cross": (4, 0, 2),
    "cproj": (4, 0, 4), "ln3": (4, 0, 6),
    "cols_b": (4, 0, 7), "rows_b": (4, 0, 3), "t3": (4, 0, 9), "xm": (4, 0, 12),
    "mlp1_0": (4, 0, 11), "mlp1_1": (4, 0, 12), "mlp1_2": (4, 0, 13), "mlp1_3": (4, 0, 13),
    "mlp2_0": (4, 1, 5), "mlp2_1": (4, 1, 8), "mlp2_2": (4, 1, 11), "mlp2_3": (4, 1, 13), "store": (4, 1, 15),
}
DENSE = {"m_cross": 1, "qc": 0, "cproj": 1, "tc": 0, "kc": 1, "t3": 0,
         "mlp1_0": 1, "mlp1_1": 0, "mlp1_2": 1, "mlp1_3": 0, "vc": 1,
         "m_self": 0, "t1": 1, "proj": 0, "mlp2": 1, "q": 0, "k": 0, "v": 0, "t2": 0}
MAX_LAG = {"self": 0, "cross": 2}
EXP_LAG = {"self": 0, "cross": 3}
EXP_START = 5
FIRST, LAST = -1, 36
LOOP_FROM, LOOP_TO = 3, 15


class Batch:

    def __init__(self, pair, u):
        self.pair, self.u = pair + u // 2, u % 2
        self.n = self.pair * 2 + self.u


class Iteration:
    def __init__(self, pair, u, batches):
        self.pair, self.u, self.batches = pair, u, batches
        self.known = isinstance(pair, int)

    def batch(self, lag):
        b = Batch(self.pair, self.u - lag)
        return b if not self.known or 0 <= b.n < self.batches else None

    def before(self):
        return Iteration(self.pair - (1 if self.u == 0 else 0), 1 - self.u, self.batches)


def lag_of(unit):
    return PLAN["mlp2_0" if unit == "mlp2" else unit][0]


def previous(it, order, lags, name):
    order = list(order)
    at, where = order.index(name), it
    for _ in range(7 * len(order)):
        at -= 1
        if at < 0:
            at, where = len(order) - 1, where.before()
        b = where.batch(lags[order[at]])
        if b is not None:
            return order[at], b
    return None


def block_kernel(nc, x, cond, ctx_in, W_mod, b_mod, W_qkv, b_qkv, W_proj, b_proj, W_qc, b_qc, W_kvc, b_kvc,
                 W_cproj, b_cproj, W_mlp1, b_mlp1, W_mlp2, b_mlp2, out):
    NB, T, D = x.shape
    F = W_mlp1.shape[1]
    C, FC = D // P, F // P
    NH = 16
    HD = D // NH
    assert (NB, T, D, HD, C, FC) == (32, 256, 256, 16, 2, 8)
    PAIRS = NH // 2
    KINDS = ("self", "cross")
    dense_lags = {n: lag_of(n) for n in DENSE}
    max_order, exp_order = ["self", "cross"], ["cross", "self"]

    def iterations(eng, body):
        for i in range(FIRST, 2 * LOOP_FROM):
            body(Iteration(i // 2, i % 2, NB))
        with eng.Fori(LOOP_FROM, LOOP_TO) as pair:
            body(Iteration(pair, 0, NB))
            body(Iteration(pair, 1, NB))
        for i in range(2 * LOOP_TO, LAST + 1):
            body(Iteration(i // 2, i % 2, NB))

    def slots(it, at):
        for half in range(2):
            for s in range(TILES):
                def due(step, late=0):
                    lag, h, slot = PLAN[step]
                    at_slot = (2 * lag + h) * TILES + slot + late
                    lag, h, slot = at_slot // (2 * TILES), at_slot // TILES % 2, at_slot % TILES
                    return it.batch(lag) if (h, slot) == (half, s) else None
                at(half, s, due)

    def max_tile(it, half, s):
        kind = "self" if half == 0 else "cross"
        b = it.batch(MAX_LAG[kind])
        return None if b is None else (kind, b, s)

    def exp_tile(it, half, s):
        if s >= EXP_START:
            kind, lag = ("cross", 3) if half == 0 else ("self", 0)
        else:
            kind, lag = ("self", 1) if half == 0 else ("cross", 3)
        b = it.batch(lag)
        return None if b is None else (kind, b, (s - EXP_START) % TILES)

    def av_group(it, half, s):
        for g, (h, slot) in enumerate(divmod(EXP_START + 5 + 4 * i, TILES) for i in range(4)):
            if s == slot:
                kind = "cross" if h == half else "self"
                lag = 3 if kind == "cross" else (0 if half == 1 else 1)
                b = it.batch(lag)
                return None if b is None else (kind, b, g)
        return None

    with ExitStack() as stack:
        def sb(name, shape, dt=F32):
            return stack.enter_context(nc.sbuf_tensor(name, shape, dt))

        def psum(name):
            return stack.enter_context(nc.psum_tensor(name, [P, 2, 512], F32))

        def sem(name):
            return stack.enter_context(nc.semaphore(name))

        def sems(name):
            return [sem(f"{name}_{u}") for u in range(2)]

        max_ps, exp_ps, o_ps, dense_ps = psum("max_ps"), psum("exp_ps"), psum("o_ps"), psum("dense_ps")

        w_shapes = {"qkv": (C, 3 * D), "proj": (C, D), "qc": (C, D), "kvc": (C, 2 * D), "cproj": (C, D),
                    "mlp1": (C, F), "mlp2": (FC, D)}
        w_dram = {"qkv": W_qkv, "proj": W_proj, "qc": W_qc, "kvc": W_kvc, "cproj": W_cproj,
                  "mlp1": W_mlp1, "mlp2": W_mlp2}
        w_hi = {n: sb(f"{n}_hi", [P, *s], F16) for n, s in w_shapes.items()}
        w_lo = {n: sb(f"{n}_lo", [P, *s], F16) for n, s in w_shapes.items()}

        ident = sb("ident", [P, P])
        ident16 = sb("ident16", [P, P], F16)
        neg_half = sb("neg_half", [P, 2])
        bc_rows = sb("bc_rows", [P, D])
        cols_a_all = sb("cols_a_all", [P, NB, 6])
        cols_b_all = sb("cols_b_all", [P, NB, C + FC])
        cols_c = sb("cols_c", [P, 2 * C])

        X = sb("X", [P, 2, 2, D])
        Ctx = sb("Ctx", [P, 2, D])
        XR = sb("XR", [P, 2, D])
        X2 = sb("X2", [P, 2, 2, D])
        XC = sb("XC", [P, 2, 2, D])
        X3 = sb("X3", [P, 2, D])
        Y = sb("Y", [P, 2, D])
        LN = ("1", "2", "c", "3")
        xn = {k: sb(f"xn{k}", [P, 2, D]) for k in LN}
        stats = {k: sb(f"stats{k}", [P, 2, 6]) for k in LN}
        mv = {k: sb(f"mv{k}", [P, 2, 2]) for k in LN}
        ve = {k: sb(f"ve{k}", [P, 2]) for k in LN}
        nm = {k: sb(f"nm{k}", [P, 2]) for k in LN}
        rs = {k: sb(f"rs{k}", [P, 2]) for k in LN}
        xt = {k: sb(f"xt{k}", [P, 2, C, T], F16) for k in LN}
        cols_a = sb("cols_a", [P, 2, 6])
        cols_b = sb("cols_b", [P, C + FC])
        rows_a = sb("rows_a", [P, 2, D])
        rows_b = sb("rows_b", [P, 2, D])
        split = {n: sb(f"split_{n}", [P, 2, C, T], F16) for n in ("q", "k", "qc", "kc")}
        q_stack = {k: sb(f"q_stack_{k}", [P, 2, PAIRS, 2 * T], F16) for k in KINDS}
        k_stack = {k: sb(f"k_stack_{k}", [P, 2, PAIRS, T], F16) for k in KINDS}
        V = {k: sb(f"V_{k}", [P, 2, 2, NH, 2 * HD]) for k in KINDS}
        mx = {k: sb(f"mx_{k}", [P, 2, 2, PAIRS]) for k in KINDS}
        mh = {k: sb(f"mh_{k}", [P, 2, 2, 2, PAIRS], F16) for k in KINDS}
        mt = {k: sb(f"mt_{k}", [32, T], F16) for k in KINDS}
        probs = sb("probs", [P, 8, 2 * T])
        o_sb = {k: sb(f"o_sb_{k}", [P, 2, 2 * T]) for k in KINDS}
        o_n = {k: sb(f"o_n_{k}", [P, C, T]) for k in KINDS}
        o_d = {k: sb(f"o_d_{k}", [P, 32]) for k in KINDS}
        o_r = {k: sb(f"o_r_{k}", [P, 32]) for k in KINDS}
        o_rb = {k: sb(f"o_rb_{k}", [P, C, T]) for k in KINDS}
        ot = {k: sb(f"ot_{k}", [P, 2, C, T], F16) for k in KINDS}
        G = sb("G", [P, FC, T])
        g_split = sb("g_split", [P, 2, FC, T], F16)

        def dram(name, shape, dt=F32):
            return nc.dram_tensor(name, shape, dt, kind="Internal").ap()

        spill = {n: dram(f"spill_{n}", [2, 2, NH, HD, T], F16) for n in split}
        zero_dram = dram("zero_dram", [32, PAIRS * 2 * T], F16)
        o_dram = {k: dram(f"o_dram_{k}", [2, 4, 2, HD, 2, C, T]) for k in KINDS}
        r_dram = {k: dram(f"r_dram_{k}", [2, 4, 2, C * T]) for k in KINDS}
        rows_a_dram, rows_b_dram = dram("rows_a_dram", [NB, 2, D]), dram("rows_b_dram", [NB, 2, D])
        bc_dram = dram("bc_dram", [1, D])

        ready = {n: sem(f"ready_{n}") for n in DENSE}
        taken = {n: sem(f"taken_{n}") for n in DENSE}
        max_ready = {k: sem(f"max_ready_{k}") for k in KINDS}
        max_taken = {k: sem(f"max_taken_{k}") for k in KINDS}
        exp_ready = {k: sem(f"exp_ready_{k}") for k in KINDS}
        exp_taken = {k: sem(f"exp_taken_{k}") for k in KINDS}
        av_done = {k: sem(f"av_done_{k}") for k in KINDS}
        mh_step = {k: sem(f"mh_step_{k}") for k in KINDS}
        o_copied = {k: sem(f"o_copied_{k}") for k in KINDS}
        o_recip = {k: sem(f"o_recip_{k}") for k in KINDS}
        o_mult = {k: sem(f"o_mult_{k}") for k in KINDS}
        ot_hi, ot_lo = ({k: sem(f"{n}_{k}") for k in KINDS} for n in ("ot_hi", "ot_lo"))
        stats_done, mv_done = ({k: sem(f"{n}_{k}") for k in LN} for n in ("stats", "mv"))
        norm_step = {k: sem(f"norm_step_{k}") for k in LN}
        hi_done = {n: sem(f"hi_{n}") for n in ("t1", "t2", "tc", "t3", "q", "k", "qc", "kc")}
        g_hi, g_lo = sem("g_hi"), sem("g_lo")
        cols_a_set, cols_b_set = sem("cols_a_set"), sem("cols_b_set")
        xr_done, xc_done, xm_done = sem("xr_done"), sem("xc_done"), sem("xm_done")
        x2_done, y_done = sem("x2_done"), sem("y_done")
        x_in, c_in, stored = sems("x_in"), sems("c_in"), sems("stored")
        rows_a_in, rows_b_in = sems("rows_a_in"), sems("rows_b_in")
        spilled = {n: sems(f"spilled_{n}") for n in split}
        stacked = {n: sems(f"stacked_{n}") for n in split}
        mrow_in = {k: sems(f"mrow_{k}") for k in KINDS}
        o_out, o_n_in, o_d_in, r_out, o_rb_in = (
            {k: sems(f"{n}_{k}") for k in KINDS} for n in ("o_out", "o_n_in", "o_d_in", "r_out", "o_rb_in"))
        passed = sem("passed")
        setup_in, w_in = sem("setup_in"), sems("w_in")
        w_hi_done, w_lo_done = sem("w_hi_done"), sem("w_lo_done")
        zeroed, ident_made, consts = sem("zeroed"), sem("ident_made"), sem("consts")
        pe_set, dve_set, act_set, sp_set = sem("pe_set"), sem("dve_set"), sem("act_set"), sem("sp_set")

        QKV_OF = {"q": "self", "k": "self", "qc": "cross", "kc": "cross"}

        def dmas(b, n):
            return (b.pair + 1) * (16 * n)

        def wait_dmas_before(eng, pair_of_sems, b, n):
            if isinstance(b.n, int) and b.n == 0:
                return
            eng.wait_ge(pair_of_sems[1 - b.u], dmas(Batch(b.pair, b.u - 1), n))

        def wait_count(eng, s, value):
            if not isinstance(value, int) or value > 0:
                eng.wait_ge(s, value)

        def apart(eng):
            eng.sem_inc(passed, 1)

        staging = (G, probs)
        w_list = list(w_shapes)

        def staged(i):
            k, n = w_shapes[w_list[i]]
            if i % 2 == 0:
                flat = G[:].rearrange("p a b -> p (a b)")
            else:
                flat = probs[:].rearrange("p a b -> p (a b)")
            return flat[:, 0:k * n].rearrange("p (k n) -> p k n", k=k)

        W_SPLITS = {"qkv": [(slice(0, D), HD ** -0.5), (slice(D, 3 * D), 1.0)], "qc": [(slice(0, D), HD ** -0.5)]}

        def w_parts(name):
            return W_SPLITS.get(name, [(slice(0, w_shapes[name][1]), 1.0)])

        q_flat = q_stack["self"][:].rearrange("p u a b -> p (u a b)")
        room = q_stack["cross"][:].rearrange("p u a b -> p (u a b)").bitcast(F32)
        MOD = room[0:NB, 0:6 * D]
        b_mod_rows = room[0:NB, 6 * D:12 * D]
        room2 = k_stack["cross"][:].rearrange("p u a b -> p (u a b)").bitcast(F32)
        cnd, cexp, cden, crec = (room2[0:NB, i * D:(i + 1) * D] for i in range(4))
        csil, v_bias = room2[0:NB, 4 * D:5 * D], room2[0:NB, 5 * D:6 * D]
        wm = V["self"][:].rearrange("p u t h d -> p (u t h d)")
        wm2 = V["cross"][:].rearrange("p u t h d -> p (u t h d)")
        room3 = k_stack["self"][:].rearrange("p u a b -> p (u a b)").bitcast(F32)
        b_rows = {n: room3[0:NB, i * D:(i + 1) * D] for i, n in enumerate(("v", "proj", "cproj", "mlp2"))}
        gb_a, gb_m = room3[0:NB, 4 * D:5 * D], room3[0:NB, 5 * D:6 * D]
        bc_row = room3[0:NB, 6 * D:7 * D]
        cT = sb("cT", [P, C, NB])
        shT = sb("shT", [P, 2, 4, NB], F16)
        vbT = sb("vbT", [P, 2, C, NB], F16)
        vcT = sb("vcT", [P, 2, C, NB], F16)
        vc_wide = sb("vc_wide", [P, C, NB])
        b_qk_col = sb("b_qk_col", [P, 2 * C])
        b_m1_col = sb("b_m1_col", [P, FC])
        b_kvc_col = sb("b_kvc_col", [P, 2 * C])

        def three(eng, dst, a_hi, a_lo, b_hi, b_lo, first=True, last=True):
            eng.matmul(dst, a_hi, b_hi, start=first, stop=False)
            eng.matmul(dst, a_hi, b_lo, start=False, stop=False)
            return eng.matmul(dst, a_lo, b_hi, start=False, stop=last)

        nonc = stack.enter_context(nc.allow_non_contiguous_dma(reason="bias columns, stacked heads"))
        block = stack.enter_context(nc.Block())

        @block.sync
        def _(sp):
            nc.sync.dma_start(cnd, cond).then_inc(setup_in, 16)
            nc.sync.dma_start(b_mod_rows, bass.AP(tensor=b_mod.tensor, offset=0, ap=[[0, NB], [1, 6 * D]])
                              ).then_inc(setup_in, 16)
            wm_dram = W_mod.rearrange("(c p) n -> p c n", p=P)
            nc.sync.dma_start(wm[:, 0:6 * D], wm_dram[:, 0]).then_inc(setup_in, 16)
            nc.sync.dma_start(wm2[:, 0:6 * D], wm_dram[:, 1]).then_inc(setup_in, 16)
            for name, src, start in (("v", b_qkv, 2 * D), ("proj", b_proj, 0), ("cproj", b_cproj, 0), ("mlp2", b_mlp2, 0)):
                nc.sync.dma_start(b_rows[name], bass.AP(tensor=src.tensor, offset=start, ap=[[0, NB], [1, D]])
                                  ).then_inc(setup_in, 16)
            nc.sync.dma_start(b_qk_col[:], b_qkv.rearrange("(c p) -> p c", p=P)[:, 0:2 * C]).then_inc(setup_in, 16)
            nc.sync.dma_start(b_m1_col[:], b_mlp1.rearrange("(c p) -> p c", p=P)).then_inc(setup_in, 16)
            nc.sync.dma_start(cols_c[:, 0:C], b_qc.rearrange("(c p) -> p c", p=P)).then_inc(setup_in, 16)
            nc.sync.dma_start(b_kvc_col[:], b_kvc.rearrange("(c p) -> p c", p=P)).then_inc(setup_in, 16)
            for i, name in enumerate(w_list):
                if i >= 2:
                    sp.wait_ge(w_lo_done, i - 1)
                nc.sync.dma_start(staged(i), w_dram[name].rearrange("(k p) n -> p k n", p=P)).then_inc(w_in[i % 2], 16)
            sp.wait_ge(zeroed, 1)
            nc.sync.dma_start(zero_dram, q_flat[0:32, 0:PAIRS * 2 * T]).then_inc(sp_set, 16)
            sp.wait_ge(dve_set, 11)
            nc.sync.dma_start(rows_a_dram[:, 0], MOD[:, 2 * D:3 * D]).then_inc(sp_set, 16)
            nc.sync.dma_start(rows_b_dram[:, 0], MOD[:, 5 * D:6 * D]).then_inc(sp_set, 16)
            nc.sync.dma_start(rows_a_dram[:, 1], gb_a).then_inc(sp_set, 16)
            nc.sync.dma_start(rows_b_dram[:, 1], gb_m).then_inc(sp_set, 16)
            nc.sync.dma_start(bc_dram, bc_row[0:1]).then_inc(sp_set, 16)
            sp.wait_ge(sp_set, 16 * 6)
            nc.sync.dma_start(bc_rows[:], bass.AP(tensor=bc_dram.tensor, offset=0, ap=[[0, P], [1, D]])).then_inc(sp_set, 16)

            def sp_wait(s, value):
                if not isinstance(value, int) or value > 0:
                    sp.wait_ge(s, value)
                    apart(sp)

            def load_x(b):
                sp_wait(xr_done, b.n - 1)
                sp_wait(norm_step["1"], (b.n - 1) * 3)
                nc.sync.dma_start(X[:, b.u], x[bass.ds(b.n, 1)].rearrange("a (t p) d -> p (a t) d", p=P)
                                  ).then_inc(x_in[b.u], 16)

            def load_c(b):
                sp_wait(norm_step["c"], b.n * 3)
                nc.sync.dma_start(Ctx[:], ctx_in[bass.ds(b.n, 1)].rearrange("a (t p) d -> p (a t) d", p=P)
                                  ).then_inc(c_in[b.u], 16)

            def load_rows(b, dst, src, s):
                row = src[bass.ds(b.n, 1)].rearrange("a r d -> a (r d)")
                nc.sync.dma_start(dst[:].rearrange("p r d -> p (r d)"), row.to_broadcast([P, 2 * D])
                                  ).then_inc(s[b.u], 16)

            def do_spill(b, n):
                sp_wait(taken[n], b.n + 1)
                nc.sync.dma_start(spill[n][b.u].rearrange("s (c h) d t -> (h d) s c t", c=C), split[n][:]
                                  ).then_inc(spilled[n][b.u], 16)

            def do_stack(b, n):
                kind = QKV_OF[n]
                sp_wait(spilled[n][b.u], dmas(b, 1))
                sp_wait(exp_ready[kind], (b.n - 1) * TILES)
                for part in range(3):
                    rows = slice(32 * part, 32 * part + 32)
                    if n[0] == "k":
                        src = spill[n][b.u, (1, 1, 0)[part]].rearrange("(p a) d t -> (a d) p t", a=2)
                        nc.sync.dma_start(k_stack[kind][rows, b.u], src).then_inc(stacked[n][b.u], 16)
                        continue
                    for ab in range(2):
                        src = spill[n][b.u, (0, 1, 1)[part]].rearrange("(p a) d t -> a d p t", a=2)[ab]
                        nc.sync.dma_start(q_stack[kind][32 * part + HD * ab:32 * part + HD * ab + HD, b.u, :, ab * T:(ab + 1) * T],
                                          src).then_inc(stacked[n][b.u], 16)
                if n[0] == "q":
                    nc.sync.dma_start(q_stack[kind][96:128, b.u].rearrange("p r t -> p (r t)"), zero_dram
                                      ).then_inc(stacked[n][b.u], 16)

            def mrow(b, kind):
                sp_wait(taken[f"m_{kind}"], b.n + 1)
                for ab in range(2):
                    nc.sync.dma_start(q_stack[kind][96 + 16 * ab:98 + 16 * ab, b.u, :, ab * T:(ab + 1) * T],
                                      mt[kind][16 * ab:16 * ab + 16]).then_inc(mrow_in[kind][b.u], 16)

            def o_store(b, kind, i):
                sp_wait(o_copied[kind], b.n * 2 + i + 1)
                nc.sync.dma_start(o_dram[kind][b.u].rearrange("j n d g c q -> (j n d) g c q")[:, :, i],
                                  o_sb[kind][:, i].rearrange("p (g q) -> p g q", g=2)).then_inc(o_out[kind][b.u], 16)

            def o_gather(b, kind):
                sp_wait(o_out[kind][b.u], dmas(b, 2))
                den = o_dram[kind][b.u][:, 1, 0].rearrange("j g c q -> j (g c q)").rearrange("j (a e) -> j a e", e=32)
                sp_wait(o_recip[kind], b.n)
                nc.sync.dma_start(o_d[kind][:], den).then_inc(o_d_in[kind][b.u], 16)
                sp_wait(ot_lo[kind], b.n)
                for gg in range(2):
                    num = o_dram[kind][b.u][:, 0].rearrange("j d g c q -> g j d (c q)")[gg]
                    nc.sync.dma_start(o_n[kind][64 * gg:64 * gg + 64].rearrange("p c q -> p (c q)"), num).then_inc(o_n_in[kind][b.u], 16)

            def r_store(b, kind):
                sp_wait(o_recip[kind], b.n + 1)
                flat = r_dram[kind][b.u].rearrange("j g (a e) -> (j g a) e", e=32)
                nc.sync.dma_start(flat, o_r[kind][:]).then_inc(r_out[kind][b.u], 16)

            def r_fetch(b, kind):
                sp_wait(r_out[kind][b.u], dmas(b, 1))
                sp_wait(o_mult[kind], b.n)
                for gg in range(2):
                    src = r_dram[kind][b.u, :, gg]
                    (j_step, j_n), (e_step, e_n) = [tuple(v) for v in src.ap]
                    nc.sync.dma_start(o_rb[kind][64 * gg:64 * gg + 64].rearrange("p c q -> p (c q)"),
                                      bass.AP(tensor=src.tensor, offset=src.offset,
                                              ap=[[j_step, j_n], [0, HD], [e_step, e_n]])).then_inc(o_rb_in[kind][b.u], 16)

            def store(b):
                sp_wait(y_done, b.n + 1)
                nc.sync.dma_start(out[bass.ds(b.n, 1)].rearrange("a (t p) d -> p (a t) d", p=P), Y[:]
                                  ).then_inc(stored[b.u], 16)

            def body(it):
                def at(half, s, due):
                    if (b := due("load_x")):
                        load_x(b)
                    if (b := due("rows_a")):
                        sp_wait(taken["proj"], b.n)
                        load_rows(b, rows_a, rows_a_dram, rows_a_in)
                    if (b := due("rows_b")):
                        sp_wait(taken["mlp2"], b.n)
                        load_rows(b, rows_b, rows_b_dram, rows_b_in)
                    if (b := due("load_c")):
                        load_c(b)
                    for kind in KINDS:
                        if (b := due(f"m_copy_{kind}")):
                            mrow(b, kind)
                    for n in split:
                        if (b := due(f"spill_{n}")):
                            do_spill(b, n)
                        if (b := due(f"stack_{n}")):
                            do_stack(b, n)
                    for kind in KINDS:
                        for i in range(2):
                            if (b := due(f"o_store{i}_{kind}")):
                                o_store(b, kind, i)
                        if (b := due(f"o_gather_{kind}")):
                            o_gather(b, kind)
                        if (b := due(f"r_out_{kind}")):
                            r_store(b, kind)
                        if (b := due(f"r_back_{kind}")):
                            r_fetch(b, kind)
                    if (b := due("store")):
                        store(b)
                slots(it, at)

            iterations(sp, body)
            for u in range(2):
                sp.wait_ge(stored[u], 16 * NB // 2)

        @block.tensor
        def _(pe):
            pe.wait_ge(ident_made, 1)
            pe.wait_ge(dve_set, 1)
            for c in range(C):
                mm = pe.transpose(dense_ps[:, 0, c * NB:(c + 1) * NB], csil[:, c * P:(c + 1) * P], ident[0:NB, 0:NB])
            mm.then_inc(pe_set, 1)
            pe.wait_ge(dve_set, 2)
            for i in range(3):
                dst = (max_ps, max_ps, exp_ps)[i][0:NB, i % 2]
                for c in range(C):
                    mm = pe.matmul(dst, cT[:, c], (wm, wm2)[c][:, i * 512:(i + 1) * 512], start=c == 0, stop=c == C - 1)
            mm.then_inc(pe_set, 1)
            pe.wait_ge(dve_set, 3)
            for i, part in enumerate((0, 1, 3, 4)):
                for c in range(C):
                    mm = pe.transpose(dense_ps[:, 1, (2 * i + c) * NB:(2 * i + c + 1) * NB],
                                      MOD[:, part * D + c * P:part * D + (c + 1) * P], ident[0:NB, 0:NB])
            mm.then_inc(pe_set, 1)
            pe.wait_ge(dve_set, 5)
            pe.wait_ge(w_lo_done, len(w_list))
            sh = lambda part, lo, c: shT[:, lo, 2 * part + c]
            for m in range(2 * C):
                for c in range(C):
                    w = slice(m * P, (m + 1) * P)
                    three(pe, dense_ps[:, 0, m * NB:(m + 1) * NB], w_hi["qkv"][:, c, w], w_lo["qkv"][:, c, w],
                          sh(0, 0, c), sh(0, 1, c), c == 0, c == C - 1)
            for m in range(FC):
                for c in range(C):
                    w = slice(m * P, (m + 1) * P)
                    three(pe, max_ps[:, 0, m * NB:(m + 1) * NB], w_hi["mlp1"][:, c, w], w_lo["mlp1"][:, c, w],
                          sh(1, 0, c), sh(1, 1, c), c == 0, c == C - 1)
            for c in range(C):
                w = slice(2 * D, 3 * D)
                mm = three(pe, max_ps[0:NB, 1, 0:D], sh(0, 0, c), sh(0, 1, c), w_hi["qkv"][:, c, w],
                           w_lo["qkv"][:, c, w], c == 0, c == C - 1)
            mm.then_inc(pe_set, 1)
            pe.wait_ge(dve_set, 7)
            for c in range(C):
                pe.transpose(dense_ps[:, 1, c * NB:(c + 1) * NB], v_bias[:, c * P:(c + 1) * P], ident[0:NB, 0:NB]
                             ).then_inc(pe_set, 1)
            for c in range(C):
                mm = three(pe, exp_ps[0:NB, 0, 0:D], vcT[:, 0, c], vcT[:, 1, c], w_hi["cproj"][:, c],
                           w_lo["cproj"][:, c], c == 0, c == C - 1)
            mm.then_inc(pe_set, 1)
            pe.wait_ge(dve_set, 9)
            for c in range(C):
                mm = three(pe, exp_ps[0:NB, 1, 0:D], vbT[:, 0, c], vbT[:, 1, c], w_hi["proj"][:, c],
                           w_lo["proj"][:, c], c == 0, c == C - 1)
            mm.then_inc(pe_set, 1)
            pe.wait_ge(dve_set, 11)
            pe.wait_ge(consts, 1)

            def tenant(it, unit):
                mates = [n for n in DENSE if DENSE[n] == DENSE[unit]]
                if (prev := previous(it, mates, dense_lags, unit)):
                    pe.wait_ge(taken[prev[0]], prev[1].n + 1)
                return dense_ps[:, DENSE[unit]]

            def turn(it, b, unit, k):
                pe.wait_ge(norm_step[k], b.n * 3 + 3)
                ps = tenant(it, unit)
                for c in range(C):
                    for t in range(2):
                        mm = pe.transpose(ps[:, c * T + t * P:c * T + (t + 1) * P], xn[k][:, t, c * P:(c + 1) * P], ident[:])
                mm.then_inc(ready[unit], 1)

            def features_out(it, unit, src, name, col):
                ps = tenant(it, unit)
                for m in range(2):
                    for c in range(C):
                        w = slice(col + m * P, col + (m + 1) * P)
                        mm = three(pe, ps[:, m * T:(m + 1) * T], w_hi[name][:, c, w], w_lo[name][:, c, w],
                                   src[:, 0, c], src[:, 1, c], c == 0, c == C - 1)
                mm.then_inc(ready[unit], 1)

            def tokens_out(it, unit, src, name, col):
                ps = tenant(it, unit)
                for t in range(2):
                    tok = slice(t * P, (t + 1) * P)
                    for c in range(C):
                        mm = three(pe, ps[:, t * D:(t + 1) * D], src[:, 0, c, tok], src[:, 1, c, tok],
                                   w_hi[name][:, c, col:col + D], w_lo[name][:, c, col:col + D], c == 0, c == C - 1)
                mm.then_inc(ready[unit], 1)

            def turn_maxima(it, b, kind):
                pe.wait_ge(mh_step[kind], b.n * 2 + 2)
                ps = tenant(it, f"m_{kind}")
                for qt in range(2):
                    mm = pe.transpose(ps[0:32, 0:P].bitcast(F16)[:, qt * P:(qt + 1) * P],
                                      mh[kind][:, qt].rearrange("p a s r -> p (a s r)"), ident16[:])
                mm.then_inc(ready[f"m_{kind}"], 1)

            def mlp2_part(it, b, part):
                t, half = part // 2, part % 2
                if part == 0:
                    pe.wait_ge(g_lo, b.n * 4 + 4)
                    tenant(it, "mlp2")
                ps = dense_ps[:, DENSE["mlp2"]]
                tok = slice(t * P, (t + 1) * P)
                for f in range(half * FC // 2, (half + 1) * FC // 2):
                    mm = three(pe, ps[:, t * D:(t + 1) * D], g_split[:, 0, f, tok], g_split[:, 1, f, tok],
                               w_hi["mlp2"][:, f], w_lo["mlp2"][:, f], f == 0, f == FC - 1)
                if part == 3:
                    mm.then_inc(ready["mlp2"], 1)

            def maxima(it, kind, b, t):
                p, qt = t // 2, t % 2
                if t == 0:
                    for n in (("q", "k") if kind == "self" else ("qc", "kc")):
                        pe.wait_ge(stacked[n][b.u], dmas(b, 7 if n[0] == "q" else 3))
                if t >= 2:
                    pe.wait_ge(max_taken[kind], b.n * TILES + t - 1)
                elif (prev := previous(it, max_order, MAX_LAG, kind)):
                    pe.wait_ge(max_taken[prev[0]], prev[1].n * TILES + TILES - 1 + t)
                for ab in range(2):
                    mm = pe.matmul(max_ps[:, t % 2, ab * T:(ab + 1) * T],
                                   q_stack[kind][:, b.u, p, ab * T + qt * P:ab * T + (qt + 1) * P],
                                   k_stack[kind][:, b.u, p], start=True, stop=True)
                mm.then_inc(max_ready[kind], 1)

            def exps(it, kind, b, t):
                p, kt = t // 2, t % 2
                if t == 0:
                    pe.wait_ge(mrow_in[kind][b.u], dmas(b, 2))
                if t >= 2:
                    pe.wait_ge(exp_taken[kind], b.n * TILES + t - 1)
                elif (prev := previous(it, exp_order, EXP_LAG, kind)):
                    pe.wait_ge(exp_taken[prev[0]], prev[1].n * TILES + TILES - 1 + t)
                pe.matmul(exp_ps[:, t % 2], k_stack[kind][:, b.u, p, kt * P:(kt + 1) * P], q_stack[kind][:, b.u, p],
                          start=True, stop=True).then_inc(exp_ready[kind], 1)

            def values(it, kind, b, g):
                pe.wait_ge(exp_taken[kind], b.n * TILES + 4 * g + 4)
                if g == 0:
                    pe.wait_ge(taken["v" if kind == "self" else "vc"], b.n + 1)
                if g % 2 == 0:
                    if (prev := previous(it, exp_order, EXP_LAG, kind)):
                        pe.wait_ge(o_copied[prev[0]], prev[1].n * 2 + g // 2 + 1)
                for kt in range(2):
                    for j in range(4):
                        tile = 4 * g + 2 * (j // 2) + kt
                        mm = pe.matmul(o_ps[32 * j:32 * j + 32, g // 2, (g % 2) * T:(g % 2 + 1) * T],
                                       V[kind][:, b.u, kt, 4 * g + j], probs[:, tile % 8, (j % 2) * T:(j % 2 + 1) * T],
                                       start=kt == 0, stop=kt == 1, tile_position=(0, 32 * j),
                                       skip_group_check=True)
                mm.then_inc(av_done[kind], 1)

            def body(it):
                def at(half, s, due):
                    if (m := max_tile(it, half, s)):
                        maxima(it, *m)
                    if (e := exp_tile(it, half, s)):
                        exps(it if (half, s >= EXP_START) != (0, False) else it.before(), *e)
                    if (v := av_group(it, half, s)):
                        values(it if not (half == 0 and s < 9) else it.before(), *v)
                    for kind in KINDS:
                        if (b := due(f"m_{kind}")):
                            turn_maxima(it, b, kind)
                    if (b := due("qc")):
                        pe.wait_ge(taken["t2"], b.n + 1)
                        features_out(it, "qc", xt["2"], "qc", 0)
                    if (b := due("cproj")):
                        pe.wait_ge(ot_lo["cross"], b.n + 1)
                        tokens_out(it, "cproj", ot["cross"], "cproj", 0)
                    if (b := due("tc")):
                        turn(it, b, "tc", "c")
                    if (b := due("kc")):
                        pe.wait_ge(taken["tc"], b.n + 1)
                        features_out(it, "kc", xt["c"], "kvc", 0)
                    if (b := due("vc")):
                        tokens_out(it, "vc", xt["c"], "kvc", D)
                    if (b := due("t3")):
                        turn(it, b, "t3", "3")
                    for i in range(4):
                        if (b := due(f"mlp1_{i}")):
                            pe.wait_ge(taken["t3"], b.n + 1)
                            features_out(it, f"mlp1_{i}", xt["3"], "mlp1", 2 * i * P)
                    if (b := due("t1")):
                        turn(it, b, "t1", "1")
                    if (b := due("proj")):
                        pe.wait_ge(ot_lo["self"], b.n + 1)
                        tokens_out(it, "proj", ot["self"], "proj", 0)
                    for i in range(4):
                        if (b := due(f"mlp2_{i}")):
                            mlp2_part(it, b, i)
                    if (b := due("q")):
                        pe.wait_ge(taken["t1"], b.n + 1)
                        features_out(it, "q", xt["1"], "qkv", 0)
                    if (b := due("k")):
                        features_out(it, "k", xt["1"], "qkv", D)
                    if (b := due("v")):
                        tokens_out(it, "v", xt["1"], "qkv", 2 * D)
                    if (b := due("t2")):
                        turn(it, b, "t2", "2")
                slots(it, at)

            iterations(pe, body)

        @block.scalar
        def _(act):
            act.wait_ge(setup_in, 16 * 12)
            nc.scalar.activation(cexp, cnd, ACT.Exp, scale=-1.0).then_inc(act_set, 1)
            for i, name in enumerate(w_list):
                act.wait_ge(w_in[i % 2], 16 * (i // 2 + 1))
                for cols, scale in w_parts(name):
                    last = nc.scalar.activation(w_hi[name][:, :, cols], staged(i)[:, :, cols], ACT.Copy, scale=scale)
                last.then_inc(w_hi_done, 1)

            def turn_hi(b, unit, k, scales):
                act.wait_ge(ready[unit], b.n + 1)
                reader = {"1": "v", "2": "qc", "c": "vc", "3": "mlp1_3"}[k]
                wait_count(act, ready[reader], b.n)
                if scales is None:
                    last = nc.scalar.activation(xt[k][:, 0].rearrange("p c t -> p (c t)"), bank(unit), ACT.Copy)
                else:
                    for c in range(C):
                        last = nc.scalar.activation(xt[k][:, 0, c], bank(unit)[:, c * T:(c + 1) * T], ACT.Copy,
                                                    scale=scales[c])
                last.then_inc(hi_done[unit], 1)

            def bank(unit):
                return dense_ps[:, DENSE[unit]]

            def project_hi(b, n, biases):
                act.wait_ge(ready[n], b.n + 1)
                wait_dmas_before(act, spilled[n], b, 1)
                for c in range(C):
                    last = nc.scalar.activation(split[n][:, 1, c], bank(n)[:, c * T:(c + 1) * T], ACT.Identity,
                                                bias=biases[c])
                last.then_inc(hi_done[n], 1)

            def keep_values(b, unit, kind):
                act.wait_ge(ready[unit], b.n + 1)
                wait_count(act, av_done[kind], (b.n - 1) * 4)
                nc.scalar.activation(V[kind][:, b.u].rearrange("p t h e -> p (t h) e")[:, :, 0:HD],
                                     bank(unit).rearrange("p (h e) -> p h e", e=HD), ACT.Copy).then_inc(taken[unit], 1)

            act.wait_ge(consts, 1)

            def body(it):
                def at(half, s, due):
                    if (e := exp_tile(it, half, s)):
                        kind, b, t = e
                        act.wait_ge(exp_ready[kind], b.n * TILES + t + 1)
                        if t >= 8:
                            act.wait_ge(av_done[kind], b.n * 4 + t // 4 - 1)
                        else:
                            src = it if (half, s >= EXP_START) != (0, False) else it.before()
                            if (prev := previous(src, exp_order, EXP_LAG, kind)):
                                act.wait_ge(av_done[prev[0]], prev[1].n * 4 + t // 4 + 3)
                        nc.scalar.activation(probs[:, t % 8], exp_ps[:, t % 2], ACT.Exp).then_inc(exp_taken[kind], 1)
                    if (v := av_group(it, half, s)) and v[2] % 2 == 1:
                        kind, b, g = v
                        act.wait_ge(av_done[kind], b.n * 4 + g + 1)
                        wait_dmas_before(act, o_out[kind], b, 2)
                        nc.scalar.activation(o_sb[kind][:, g // 2], o_ps[:, g // 2], ACT.Copy).then_inc(o_copied[kind], 1)
                    if (b := due("tc")):
                        turn_hi(b, "tc", "c", None)
                    if (b := due("kc")):
                        project_hi(b, "kc", [cols_c[:, C + c:C + c + 1] for c in range(C)])
                    if (b := due("vc")):
                        keep_values(b, "vc", "cross")
                    if (b := due("t3")):
                        act.wait_ge(cols_b_set, b.n + 1)
                        turn_hi(b, "t3", "3", [cols_b[:, c:c + 1] for c in range(C)])
                    if (b := due("mlp1_1")):
                        wait_count(act, g_lo, b.n * 4)
                        for i in range(4):
                            act.wait_ge(ready[f"mlp1_{i}"], b.n + 1)
                            for m in range(2):
                                f = 2 * i + m
                                last = nc.scalar.activation(G[:, f], bank(f"mlp1_{i}")[:, m * T:(m + 1) * T],
                                                            ACT.Gelu_apprx_tanh, bias=cols_b[:, C + f:C + f + 1])
                            last.then_inc(taken[f"mlp1_{i}"], 1)
                    if (b := due("t1")):
                        act.wait_ge(cols_a_set, b.n + 1)
                        turn_hi(b, "t1", "1", [cols_a[:, b.u, 4 + c:5 + c] for c in range(C)])
                    if (b := due("q")):
                        project_hi(b, "q", [cols_a[:, b.u, c:c + 1] for c in range(C)])
                    if (b := due("k")):
                        project_hi(b, "k", [cols_a[:, b.u, C + c:C + c + 1] for c in range(C)])
                    if (b := due("v")):
                        keep_values(b, "v", "self")
                    if (b := due("t2")):
                        turn_hi(b, "t2", "2", None)
                    if (b := due("qc")):
                        project_hi(b, "qc", [cols_c[:, c:c + 1] for c in range(C)])
                slots(it, at)

            iterations(act, body)

        @block.vector
        def _(dve):
            dve.wait_ge(act_set, 1)
            chain = sem("dve_chain")
            links = [0]

            def then(ins):
                links[0] += 1
                ins.then_inc(chain, 1)
                dve.wait_ge(chain, links[0])

            then(nc.vector.tensor_scalar_add(cden, cexp, 1.0))
            then(nc.vector.reciprocal(crec, cden))
            nc.vector.tensor_tensor(csil, cnd, crec, ALU.mult).then_inc(dve_set, 1)
            dve.wait_ge(pe_set, 1)
            nc.vector.tensor_copy(cT[:].rearrange("p c b -> p (c b)"), dense_ps[:, 0, 0:C * NB]).then_inc(dve_set, 1)
            dve.wait_ge(pe_set, 2)
            for i in range(3):
                last = nc.vector.tensor_tensor(MOD[:, i * 512:(i + 1) * 512], (max_ps, max_ps, exp_ps)[i][0:NB, i % 2],
                                               b_mod_rows[:, i * 512:(i + 1) * 512], ALU.add)
            last.then_inc(dve_set, 1)
            dve.wait_ge(pe_set, 3)
            turned = dense_ps[:, 1, 0:8 * NB].rearrange("p (i c b) -> p i c b", i=4, c=C)
            for i, dst in ((1, cols_a_all[:, :, 4:6]), (3, cols_b_all[:, :, 0:C])):
                nc.vector.tensor_scalar_add(dst.rearrange("p b c -> p c b"), turned[:, i], 1.0)
            for part, i in ((0, 0), (1, 2)):
                last = nc.vector.tensor_copy(shT[:, 0, 2 * part:2 * part + 2], turned[:, i])
            last.then_inc(dve_set, 1)
            dve.wait_ge(dve_set, 4)
            for part, i in ((0, 0), (1, 2)):
                last = nc.vector.tensor_tensor(shT[:, 1, 2 * part:2 * part + 2], turned[:, i],
                                               shT[:, 0, 2 * part:2 * part + 2], ALU.subtract)
            last.then_inc(dve_set, 1)
            for i, name in enumerate(w_list):
                dve.wait_ge(w_hi_done, i + 1)
                for cols, scale in w_parts(name):
                    last = nc.vector.scalar_tensor_tensor(out=w_lo[name][:, :, cols], in0=staged(i)[:, :, cols], scalar=scale,
                                                          in1=w_hi[name][:, :, cols], op0=ALU.mult, op1=ALU.subtract)
                last.then_inc(w_lo_done, 1)
            then(nc.vector.tensor_scalar_mul(b_qk_col[:, 0:C], b_qk_col[:, 0:C], HD ** -0.5))
            nc.vector.tensor_scalar_mul(cols_c[:, 0:C], cols_c[:, 0:C], HD ** -0.5)
            nc.vector.tensor_copy(cols_c[:, C:2 * C], b_kvc_col[:, 0:C])
            then(nc.vector.memset(vc_wide[:], 0.0))
            for c in range(C):
                last = nc.vector.tensor_scalar_add(vc_wide[:, c], vc_wide[:, c], b_kvc_col[:, C + c:C + c + 1])
            then(last)
            then(nc.vector.tensor_copy(vcT[:, 0], vc_wide[:]))
            nc.vector.tensor_tensor(vcT[:, 1], vc_wide[:], vcT[:, 0], ALU.subtract).then_inc(dve_set, 1)
            dve.wait_ge(pe_set, 4)
            for m in range(2 * C):
                nc.vector.tensor_scalar_add(cols_a_all[:, :, m], dense_ps[:, 0, m * NB:(m + 1) * NB], b_qk_col[:, m:m + 1])
            for m in range(FC):
                nc.vector.tensor_scalar_add(cols_b_all[:, :, C + m], max_ps[:, 0, m * NB:(m + 1) * NB], b_m1_col[:, m:m + 1])
            nc.vector.tensor_tensor(v_bias, max_ps[0:NB, 1, 0:D], b_rows["v"], ALU.add).then_inc(dve_set, 1)
            dve.wait_ge(pe_set, 6)
            vb_ps = dense_ps[:, 1, 0:C * NB].rearrange("p (c b) -> p c b", c=C)
            nc.vector.tensor_copy(vbT[:, 0], vb_ps).then_inc(dve_set, 1)
            dve.wait_ge(dve_set, 8)
            nc.vector.tensor_tensor(vbT[:, 1], vb_ps, vbT[:, 0], ALU.subtract).then_inc(dve_set, 1)
            dve.wait_ge(pe_set, 7)
            nc.vector.tensor_tensor(bc_row, exp_ps[0:NB, 0, 0:D], b_rows["cproj"], ALU.add)
            nc.vector.tensor_tensor(gb_m, MOD[:, 5 * D:6 * D], b_rows["mlp2"], ALU.mult).then_inc(dve_set, 1)
            dve.wait_ge(pe_set, 8)
            then(nc.vector.tensor_tensor(gb_a, exp_ps[0:NB, 1, 0:D], b_rows["proj"], ALU.add))
            nc.vector.tensor_tensor(gb_a, gb_a, MOD[:, 2 * D:3 * D], ALU.mult).then_inc(dve_set, 1)

            def bank(unit):
                return dense_ps[:, DENSE[unit]]

            def statistics(b, k, src):
                for t in range(2):
                    last = nc.vector.bn_stats(stats[k][:, t], src[:, t])
                last.then_inc(stats_done[k], 1)
                dve.wait_ge(stats_done[k], b.n + 1)
                wait_count(dve, norm_step[k], b.n * 3)
                apart(dve)
                for t in range(2):
                    last = nc.vector.bn_aggr(mv[k][:, t], stats[k][:, t])
                last.then_inc(mv_done[k], 1)

            def turn_lo(b, unit, k, scales):
                dve.wait_ge(hi_done[unit], b.n + 1)
                if scales is None:
                    last = nc.vector.tensor_tensor(xt[k][:, 1].rearrange("p c t -> p (c t)"), bank(unit),
                                                   xt[k][:, 0].rearrange("p c t -> p (c t)"), ALU.subtract)
                else:
                    for c in range(C):
                        last = nc.vector.scalar_tensor_tensor(out=xt[k][:, 1, c], in0=bank(unit)[:, c * T:(c + 1) * T],
                                                              scalar=scales[c], in1=xt[k][:, 0, c],
                                                              op0=ALU.mult, op1=ALU.subtract)
                last.then_inc(taken[unit], 1)

            def project_lo(b, n, biases):
                dve.wait_ge(hi_done[n], b.n + 1)
                for c in range(C):
                    last = nc.vector.scalar_tensor_tensor(out=split[n][:, 0, c], in0=bank(n)[:, c * T:(c + 1) * T],
                                                          scalar=biases[c], in1=split[n][:, 1, c],
                                                          op0=ALU.add, op1=ALU.subtract)
                last.then_inc(taken[n], 1)

            def split_maxima(b, kind):
                wait_count(dve, ready[f"m_{kind}"], b.n)
                dve.wait_ge(max_taken[kind], (b.n + 1) * TILES)
                view = mh[kind][:].rearrange("p q a s r -> p (q a) s r")
                top = mx[kind][:].rearrange("p q a r -> p (q a) r")
                nc.vector.tensor_scalar_mul(view[:, :, 0], top, -1.0 / SHIFT_UNIT).then_inc(mh_step[kind], 1)
                dve.wait_ge(mh_step[kind], b.n * 2 + 1)
                nc.vector.scalar_tensor_tensor(out=view[:, :, 1], in0=top, scalar=-1.0 / SHIFT_UNIT, in1=view[:, :, 0],
                                               op0=ALU.mult, op1=ALU.subtract).then_inc(mh_step[kind], 1)

            def body(it):
                def at(half, s, due):
                    for kind in KINDS:
                        if (b := due(f"split_{kind}")):
                            split_maxima(b, kind)
                        if (b := due(f"m_copy_{kind}")):
                            dve.wait_ge(ready[f"m_{kind}"], b.n + 1)
                            wait_dmas_before(dve, mrow_in[kind], b, 2)
                            nc.vector.tensor_copy(mt[kind][:], bank(f"m_{kind}")[0:32, 0:P].bitcast(F16)
                                                  ).then_inc(taken[f"m_{kind}"], 1)
                    if (m := max_tile(it, half, s)):
                        kind, b, t = m
                        dve.wait_ge(max_ready[kind], b.n * TILES + t + 1)
                        nc.vector.tensor_reduce(mx[kind][:, t % 2, :, t // 2],
                                                max_ps[:, t % 2].rearrange("p (a k) -> p a k", a=2), AX_X, ALU.max
                                                ).then_inc(max_taken[kind], 1)
                    if (b := due("cols_a")):
                        wait_count(dve, taken["k"], b.n - 1)
                        nc.vector.tensor_scalar_add(cols_a[:, b.u], cols_a_all[:, bass.ds(b.n, 1)].rearrange("p a c -> p (a c)"), 0.0
                                                    ).then_inc(cols_a_set, 1)
                    if (b := due("cols_b")):
                        wait_count(dve, taken["mlp1_3"], b.n)
                        nc.vector.tensor_scalar_add(cols_b[:], cols_b_all[:, bass.ds(b.n, 1)].rearrange("p a c -> p (a c)"), 0.0
                                                    ).then_inc(cols_b_set, 1)
                    if (b := due("ln1")):
                        dve.wait_ge(x_in[b.u], dmas(b, 1))
                        statistics(b, "1", X[:, b.u])
                    for kind in KINDS:
                        if (b := due(f"o_recip_{kind}")):
                            dve.wait_ge(o_d_in[kind][b.u], dmas(b, 1))
                            wait_dmas_before(dve, r_out[kind], b, 1)
                            nc.vector.reciprocal(o_r[kind][:], o_d[kind][:]).then_inc(o_recip[kind], 1)
                        if (b := due(f"o_hi_{kind}")):
                            dve.wait_ge(o_mult[kind], b.n + 1)
                            wait_count(dve, ready["proj" if kind == "self" else "cproj"], b.n)
                            nc.vector.tensor_copy(ot[kind][:, 0], o_n[kind][:]).then_inc(ot_hi[kind], 1)
                            dve.wait_ge(ot_hi[kind], b.n + 1)
                            nc.vector.tensor_tensor(ot[kind][:, 1], o_n[kind][:], ot[kind][:, 0], ALU.subtract
                                                    ).then_inc(ot_lo[kind], 1)
                    if (b := due("cproj", late=1)):
                        dve.wait_ge(ready["cproj"], b.n + 1)
                        dve.wait_ge(xc_done, b.n + 1)
                        wait_count(dve, y_done, b.n)
                        nc.vector.tensor_tensor(X3[:].rearrange("p t d -> p (t d)"), bank("cproj"),
                                                XC[:, b.u].rearrange("p t d -> p (t d)"), ALU.add).then_inc(taken["cproj"], 1)
                    if (b := due("ln3")):
                        dve.wait_ge(taken["cproj"], b.n + 1)
                        statistics(b, "3", X3)
                    if (b := due("tc", late=1)):
                        turn_lo(b, "tc", "c", None)
                    if (b := due("kc", late=1)):
                        project_lo(b, "kc", [cols_c[:, C + c:C + c + 1] for c in range(C)])
                    if (b := due("t3", late=1)):
                        turn_lo(b, "t3", "3", [cols_b[:, c:c + 1] for c in range(C)])
                    for i in range(4):
                        if (b := due("mlp1_3", late=1 + i // 2)):
                            if i == 0:
                                wait_count(dve, ready["mlp2"], b.n)
                            dve.wait_ge(taken[f"mlp1_{i}"], b.n + 1)
                            nc.vector.tensor_copy(g_split[:, 0, 2 * i:2 * i + 2], G[:, 2 * i:2 * i + 2]).then_inc(g_hi, 1)
                    if (b := due("proj", late=1)):
                        dve.wait_ge(ready["proj"], b.n + 1)
                        dve.wait_ge(rows_a_in[b.u], dmas(b, 1))
                        wait_count(dve, xc_done, b.n - 1)
                        nc.vector.tensor_tensor(X2[:, b.u], bank("proj").rearrange("p (t d) -> p t d", t=2),
                                                rows_a[:, 0:1].to_broadcast([P, 2, D]), ALU.mult).then_inc(taken["proj"], 1)
                        dve.wait_ge(taken["proj"], b.n + 1)
                        dve.wait_ge(xr_done, b.n + 1)
                        nc.vector.tensor_tensor(X2[:, b.u], X2[:, b.u], XR[:], ALU.add).then_inc(x2_done, 1)
                    if (b := due("ln2")):
                        dve.wait_ge(x2_done, b.n + 1)
                        statistics(b, "2", X2[:, b.u])
                    if (b := due("t1", late=1)):
                        turn_lo(b, "t1", "1", [cols_a[:, b.u, 4 + c:5 + c] for c in range(C)])
                    if (b := due("q", late=1)):
                        project_lo(b, "q", [cols_a[:, b.u, c:c + 1] for c in range(C)])
                    if (b := due("k", late=1)):
                        project_lo(b, "k", [cols_a[:, b.u, C + c:C + c + 1] for c in range(C)])
                    if (b := due("mlp2_3", late=1)):
                        dve.wait_ge(ready["mlp2"], b.n + 1)
                        dve.wait_ge(rows_b_in[b.u], dmas(b, 1))
                        wait_dmas_before(dve, stored, b, 1)
                        nc.vector.tensor_tensor(Y[:], bank("mlp2").rearrange("p (t d) -> p t d", t=2),
                                                rows_b[:, 0:1].to_broadcast([P, 2, D]), ALU.mult).then_inc(taken["mlp2"], 1)
                        dve.wait_ge(taken["mlp2"], b.n + 1)
                        dve.wait_ge(xm_done, b.n + 1)
                        nc.vector.tensor_tensor(Y[:], Y[:], X3[:], ALU.add).then_inc(y_done, 1)
                    if (b := due("t2", late=1)):
                        turn_lo(b, "t2", "2", None)
                    if (b := due("qc", late=1)):
                        project_lo(b, "qc", [cols_c[:, c:c + 1] for c in range(C)])
                    if (b := due("lnc")):
                        dve.wait_ge(c_in[b.u], dmas(b, 1))
                        statistics(b, "c", Ctx)
                slots(it, at)

            iterations(dve, body)

        @block.gpsimd
        def _(pool):
            nc.gpsimd.memset(ident[:], 0.0).then_inc(consts_pool := sem("ident_zero"), 1)
            pool.wait_ge(consts_pool, 1)
            nc.gpsimd.affine_select(out=ident[:], in_=ident[:], compare_op=ALU.not_equal, fill=1.0, base=0,
                                    pattern=[[-1, P]], channel_multiplier=1).then_inc(ident_made, 1)
            pool.wait_ge(ident_made, 1)
            nc.gpsimd.tensor_copy(ident16[:], ident[:])
            nc.gpsimd.memset(neg_half[:], -0.5)
            nc.gpsimd.memset(q_stack["self"][:], 0.0).then_inc(zeroed, 1)
            pool.wait_ge(sp_set, 16 * 6)
            pool.wait_ge(dve_set, 11)
            nc.gpsimd.memset(q_stack["cross"][:], 0.0)
            for kind in KINDS:
                nc.gpsimd.memset(V[kind][:], 1.0)
                last = nc.gpsimd.memset(k_stack[kind][:], SHIFT_UNIT)
            last.then_inc(consts, 1)

            def normalise(b, k, src):
                pool.wait_ge(mv_done[k], b.n + 1)
                apart(pool)
                nc.gpsimd.tensor_scalar(ve[k][:], mv[k][:, :, 1], LN_EPS, 1.0, ALU.add, ALU.mult).then_inc(norm_step[k], 1)
                nc.gpsimd.tensor_scalar(nm[k][:], mv[k][:, :, 0], -1.0, 0.0, ALU.mult, ALU.add)
                pool.wait_ge(norm_step[k], b.n * 3 + 1)
                nc.gpsimd.tensor_tensor(rs[k][:], ve[k][:], neg_half[:], ALU.pow).then_inc(norm_step[k], 1)
                pool.wait_ge(norm_step[k], b.n * 3 + 2)
                unit = {"1": "t1", "2": "t2", "c": "tc", "3": "t3"}[k]
                wait_count(pool, ready[unit], b.n)
                apart(pool)
                for t in range(2):
                    last = nc.gpsimd.tensor_scalar(xn[k][:, t], src[:, t], nm[k][:, t:t + 1], rs[k][:, t:t + 1],
                                                   ALU.add, ALU.mult)
                last.then_inc(norm_step[k], 1)

            def body(it):
                def at(half, s, due):
                    for kind in KINDS:
                        if (b := due(f"o_norm_{kind}")):
                            pool.wait_ge(o_n_in[kind][b.u], dmas(b, 2))
                            pool.wait_ge(o_rb_in[kind][b.u], dmas(b, 2))
                            nc.gpsimd.tensor_tensor(o_n[kind][:], o_n[kind][:], o_rb[kind][:], ALU.mult).then_inc(o_mult[kind], 1)
                    if (b := due("ln1")):
                        normalise(b, "1", X[:, b.u])
                    if (b := due("xr")):
                        pool.wait_ge(rows_a_in[b.u], dmas(b, 1))
                        wait_count(pool, x2_done, b.n)
                        nc.gpsimd.tensor_tensor(XR[:], X[:, b.u], rows_a[:, 1:2].to_broadcast([P, 2, D]), ALU.add
                                                ).then_inc(xr_done, 1)
                    if (b := due("xc")):
                        wait_count(pool, taken["cproj"], b.n - 1)
                        nc.gpsimd.tensor_tensor(XC[:, b.u], X2[:, b.u],
                                                bc_rows[:].rearrange("p (a d) -> p a d", a=1).to_broadcast([P, 2, D]), ALU.add
                                                ).then_inc(xc_done, 1)
                    if (b := due("xm")):
                        pool.wait_ge(taken["cproj"], b.n + 1)
                        pool.wait_ge(rows_b_in[b.u], dmas(b, 1))
                        pool.wait_ge(norm_step["3"], b.n * 3 + 3)
                        nc.gpsimd.tensor_tensor(X3[:], X3[:], rows_b[:, 1:2].to_broadcast([P, 2, D]), ALU.add
                                                ).then_inc(xm_done, 1)
                    if (b := due("ln3")):
                        normalise(b, "3", X3)
                    for i in range(4):
                        if (b := due("mlp1_3", late=4 + i // 2)):
                            pool.wait_ge(g_hi, b.n * 4 + i + 1)
                            nc.gpsimd.tensor_tensor(g_split[:, 1, 2 * i:2 * i + 2], G[:, 2 * i:2 * i + 2],
                                                    g_split[:, 0, 2 * i:2 * i + 2], ALU.subtract).then_inc(g_lo, 1)
                    if (b := due("ln2")):
                        normalise(b, "2", X2[:, b.u])
                    if (b := due("lnc")):
                        normalise(b, "c", Ctx)
                slots(it, at)

            pool.wait_ge(sp_set, 16 * 7)
            iterations(pool, body)


_INS = ["x", "cond_1024", "ctx_1024"] + [f"L0_xcond_{n}" for n in (
    "W_mod", "b_mod", "W_qkv", "b_qkv", "W_proj", "b_proj", "W_qc", "b_qc", "W_kvc", "b_kvc",
    "W_cproj", "b_cproj", "W_mlp1", "b_mlp1", "W_mlp2", "b_mlp2")]


def kernel(**inputs):
    import numpy as np
    import concourse.bacc as bacc
    from concourse.bass_utils import run_bass_kernel_spmd

    nc = bacc.Bacc("TRN2", target_bir_lowering=False, num_devices=1)
    arrays, args = {}, []
    for name in _INS:
        a = np.ascontiguousarray(inputs[name])
        arrays[f"in_{name}"] = a
        args.append(nc.dram_tensor(f"in_{name}", a.shape, mybir.dt.from_np(a.dtype), kind="ExternalInput").ap())
    args.append(nc.dram_tensor("out_x", inputs["x"].shape, F32, kind="ExternalOutput").ap())
    block_kernel(nc, *args)
    return run_bass_kernel_spmd(nc, [arrays], core_ids=[0]).results[0]["out_x"]
```

```python
from contextlib import ExitStack

import concourse.bass as bass
from concourse import mybir

F32 = mybir.dt.float32
F16 = mybir.dt.float16
ALU = mybir.AluOpType
ACT = mybir.ActivationFunctionType
AX_X = mybir.AxisListType.X

P = 128
LN_EPS = 1e-6
TILES = 16
SHIFT_UNIT = 64.0

PLAN = {
    "load_x": (-1, 0, 6), "cols_a": (-1, 0, 10), "ln1": (-1, 0, 14), "norm1": (-1, 0, 14), "t1": (-1, 1, 2),
    "t1_hi": (-1, 1, 3), "t1_lo": (-1, 1, 4), "q": (-1, 1, 7), "q_hi": (-1, 1, 7), "q_lo": (-1, 1, 8),
    "spill_q": (-1, 1, 9), "stack_q": (-1, 1, 11), "k": (-1, 1, 8), "k_hi": (-1, 1, 8), "k_lo": (-1, 1, 9),
    "spill_k": (-1, 1, 10), "stack_k": (-1, 1, 13), "v": (-1, 1, 9), "v_hi": (-1, 1, 10),
    "split_self": (0, 1, 0), "m_self": (0, 1, 0), "m_copy_self": (0, 1, 1), "o_store0_self": (1, 0, 2),
    "o_store1_self": (1, 0, 6), "o_gather_self": (1, 0, 8), "o_recip_self": (1, 0, 11),
    "r_out_self": (1, 0, 10), "r_back_self": (1, 0, 15), "o_norm_self": (1, 1, 0), "o_hi_self": (1, 1, 2),
    "rows_a": (1, 0, 1), "xr": (1, 0, 6), "proj": (1, 1, 4), "x2": (1, 1, 5),
    "ln2": (1, 1, 7), "norm2": (1, 1, 8), "t2": (1, 1, 15), "t2_hi": (1, 1, 15), "t2_lo": (2, 0, 0),
    "qc": (2, 0, 3), "qc_hi": (2, 0, 3), "qc_lo": (2, 0, 4), "spill_qc": (2, 0, 6), "stack_qc": (2, 0, 7),
    "xc": (2, 1, 8), "load_c": (1, 0, 14), "lnc": (1, 1, 4), "normc": (1, 1, 7), "tc": (1, 1, 14),
    "tc_hi": (1, 1, 14), "tc_lo": (1, 1, 15), "kc": (2, 0, 8), "kc_hi": (2, 0, 9), "kc_lo": (2, 0, 9),
    "spill_kc": (2, 0, 9), "stack_kc": (2, 0, 12), "vc": (2, 0, 14), "vc_hi": (2, 0, 15),
    "split_cross": (3, 0, 0), "m_cross": (3, 0, 1), "m_copy_cross": (3, 0, 1), "o_store0_cross": (3, 1, 0),
    "o_store1_cross": (3, 1, 5), "o_gather_cross": (3, 1, 9), "o_recip_cross": (3, 1, 11),
    "r_out_cross": (3, 1, 11), "r_back_cross": (3, 1, 13), "o_norm_cross": (3, 1, 15), "o_hi_cross": (4, 0, 3),
    "cproj": (4, 0, 4), "x3": (4, 0, 5),
    "ln3": (4, 0, 6), "norm3": (4, 0, 6), "cols_b": (4, 0, 7), "rows_b": (3, 1, 14), "t3": (4, 0, 9),
    "t3_hi": (4, 0, 9), "t3_lo": (4, 0, 10), "xm": (4, 0, 7), "mlp1_0": (4, 0, 12), "mlp1_1": (4, 0, 12),
    "mlp1_2": (4, 0, 12), "mlp1_3": (4, 0, 13), "gelu": (4, 0, 12), "g_hi_0": (4, 0, 12), "g_hi_1": (4, 0, 12),
    "g_hi_2": (4, 0, 13), "g_hi_3": (4, 0, 15), "g_lo_0": (4, 1, 1), "g_lo_1": (4, 1, 1), "g_lo_2": (4, 1, 2),
    "g_lo_3": (4, 1, 2), "mlp2_0": (4, 1, 6), "mlp2_1": (4, 1, 8), "mlp2_2": (4, 1, 11), "mlp2_3": (4, 1, 13),
    "y": (4, 1, 13), "y_add": (4, 1, 13), "store": (4, 1, 15),
}
BANK = {"m_self": 1, "m_cross": 2, "qc": 2, "cproj": 0, "tc": 1, "kc": 2, "t3": 0, "mlp1_0": 1, "mlp1_1": 2,
        "mlp1_2": 0, "mlp1_3": 1, "vc": 2, "t1": 1, "proj": 0, "mlp2": 2, "q": 1, "k": 0, "v": 1, "t2": 0}
DENSE = {n: BANK[n] for n in sorted(BANK, key=lambda n: PLAN["mlp2_0" if n == "mlp2" else n][1:])}
MAX_LAG = {"self": 0, "cross": 2}
EXP_LAG = {"self": 0, "cross": 3}
EXP_START = 5
AV_AFTER = 5
FIRST, LAST = -1, 36
LOOP_FROM, LOOP_TO = 3, 15


class Batch:

    def __init__(self, pair, u):
        self.pair, self.u = pair + u // 2, u % 2
        self.n = self.pair * 2 + self.u


class Iteration:
    def __init__(self, pair, u, batches):
        self.pair, self.u, self.batches = pair, u, batches
        self.known = isinstance(pair, int)

    def batch(self, lag):
        b = Batch(self.pair, self.u - lag)
        return b if not self.known or 0 <= b.n < self.batches else None

    def before(self):
        return Iteration(self.pair - (1 if self.u == 0 else 0), 1 - self.u, self.batches)


def lag_of(unit):
    return PLAN["mlp2_0" if unit == "mlp2" else unit][0]


def previous(it, order, lags, name):
    order = list(order)
    at, where = order.index(name), it
    for _ in range(7 * len(order)):
        at -= 1
        if at < 0:
            at, where = len(order) - 1, where.before()
        b = where.batch(lags[order[at]])
        if b is not None:
            return order[at], b
    return None


def block_kernel(nc, x, cond, ctx_in, W_mod, b_mod, W_qkv, b_qkv, W_proj, b_proj, W_qc, b_qc, W_kvc, b_kvc,
                 W_cproj, b_cproj, W_mlp1, b_mlp1, W_mlp2, b_mlp2, out):
    NB, T, D = x.shape
    F = W_mlp1.shape[1]
    C, FC = D // P, F // P
    NH = 16
    HD = D // NH
    assert (NB, T, D, HD, C, FC) == (32, 256, 256, 16, 2, 8)
    PAIRS = NH // 2
    KINDS = ("self", "cross")
    dense_lags = {n: lag_of(n) for n in DENSE}
    max_order, exp_order = ["self", "cross"], ["cross", "self"]

    def iterations(eng, body, late_setup, last_setup=None):
        for i in range(FIRST, 2 * LOOP_FROM):
            body(Iteration(i // 2, i % 2, NB))
            if i == FIRST:
                late_setup()
            if i == FIRST + 1 and last_setup:
                last_setup()
        with eng.Fori(LOOP_FROM, LOOP_TO) as pair:
            body(Iteration(pair, 0, NB))
            body(Iteration(pair, 1, NB))
        for i in range(2 * LOOP_TO, LAST + 1):
            body(Iteration(i // 2, i % 2, NB))

    def slots(it, at):
        for half in range(2):
            for s in range(TILES):
                def due(step):
                    lag, h, slot = PLAN[step]
                    return it.batch(lag) if (h, slot) == (half, s) else None
                at(half, s, due)

    def max_tile(it, half, s):
        kind = "self" if half == 0 else "cross"
        b = it.batch(MAX_LAG[kind])
        return None if b is None else (kind, b, s)

    def exp_tile(it, half, s):
        if s >= EXP_START:
            kind, lag = ("cross", 3) if half == 0 else ("self", 0)
        else:
            kind, lag = ("self", 1) if half == 0 else ("cross", 3)
        b = it.batch(lag)
        return None if b is None else (kind, b, (s - EXP_START) % TILES)

    def av_group(it, half, s):
        for g, (h, slot) in enumerate(divmod(EXP_START + AV_AFTER + 4 * i, TILES) for i in range(4)):
            if s == slot:
                kind = "cross" if h == half else "self"
                lag = 3 if kind == "cross" else (0 if half == 1 else 1)
                b = it.batch(lag)
                return None if b is None else (kind, b, g)
        return None

    with ExitStack() as stack:
        def sb(name, shape, dt=F32):
            return stack.enter_context(nc.sbuf_tensor(name, shape, dt))

        def psum(name, banks):
            return stack.enter_context(nc.psum_tensor(name, [P, banks, 512], F32))

        def sem(name):
            return stack.enter_context(nc.semaphore(name))

        def sems(name):
            return [sem(f"{name}_{u}") for u in range(2)]

        max_ps, exp_ps, o_ps, dense_ps = psum("max_ps", 2), psum("exp_ps", 2), psum("o_ps", 1), psum("dense_ps", 3)

        w_shapes = {"qkv": (C, 3 * D), "proj": (C, D), "qc": (C, D), "kvc": (C, 2 * D), "cproj": (C, D),
                    "mlp1": (C, F), "mlp2": (FC, D)}
        w_dram = {"qkv": W_qkv, "proj": W_proj, "qc": W_qc, "kvc": W_kvc, "cproj": W_cproj,
                  "mlp1": W_mlp1, "mlp2": W_mlp2}
        w_hi = {n: sb(f"{n}_hi", [P, *s], F16) for n, s in w_shapes.items()}
        w_lo = {n: sb(f"{n}_lo", [P, *s], F16) for n, s in w_shapes.items()}

        ident = sb("ident", [P, P])
        ident16 = sb("ident16", [P, P], F16)
        neg_half = sb("neg_half", [P, 2])
        bc_rows = sb("bc_rows", [P, D])
        cols_a_all = sb("cols_a_all", [P, NB, 6])
        cols_b_all = sb("cols_b_all", [P, NB, C + FC])
        cols_c = sb("cols_c", [P, 2 * C])

        X = sb("X", [P, 2, 2, D])
        Ctx = sb("Ctx", [P, 2, D])
        XR = sb("XR", [P, 2, D])
        X2 = sb("X2", [P, 2, 2, D])
        XC = sb("XC", [P, 2, 2, D])
        X3 = sb("X3", [P, 2, D])
        Y = sb("Y", [P, 2, D])
        LN = ("1", "2", "c", "3")
        xn = {k: sb(f"xn{k}", [P, 2, D]) for k in LN}
        stats = {k: sb(f"stats{k}", [P, 2, 6]) for k in LN}
        mv = {k: sb(f"mv{k}", [P, 2, 2]) for k in LN}
        ve = {k: sb(f"ve{k}", [P, 2]) for k in LN}
        nm = {k: sb(f"nm{k}", [P, 2]) for k in LN}
        rs = {k: sb(f"rs{k}", [P, 2]) for k in LN}
        xt = {k: sb(f"xt{k}", [P, 2, C, T], F16) for k in LN}
        cols_a = sb("cols_a", [P, 2, 6])
        cols_b = sb("cols_b", [P, C + FC])
        rows_a = sb("rows_a", [P, 2, D])
        rows_b = sb("rows_b", [P, 2, D])
        split = {n: sb(f"split_{n}", [P, 2, C, T], F16) for n in ("q", "k", "qc", "kc")}
        q_stack = {k: sb(f"q_stack_{k}", [P, 2, PAIRS, 2 * T], F16) for k in KINDS}
        k_stack = {k: sb(f"k_stack_{k}", [P, 2, PAIRS, T], F16) for k in KINDS}
        V = {k: sb(f"V_{k}", [P, 2, 2, NH, 2 * HD]) for k in KINDS}
        mx = {k: sb(f"mx_{k}", [P, 2, 2, PAIRS]) for k in KINDS}
        mh = {k: sb(f"mh_{k}", [P, 2, 2, 2, PAIRS], F16) for k in KINDS}
        mt = {k: sb(f"mt_{k}", [32, T], F16) for k in KINDS}
        probs = sb("probs", [P, 8, 2 * T])
        o_sb = {k: sb(f"o_sb_{k}", [P, 2, 2 * T]) for k in KINDS}
        o_n = {k: sb(f"o_n_{k}", [P, C, T]) for k in KINDS}
        o_d = {k: sb(f"o_d_{k}", [P, 32]) for k in KINDS}
        o_r = {k: sb(f"o_r_{k}", [P, 32]) for k in KINDS}
        o_rb = {k: sb(f"o_rb_{k}", [P, C, T]) for k in KINDS}
        ot = {k: sb(f"ot_{k}", [P, 2, C, T], F16) for k in KINDS}
        G = sb("G", [P, FC, T])
        g_split = sb("g_split", [P, 2, FC, T], F16)

        def dram(name, shape, dt=F32):
            return nc.dram_tensor(name, shape, dt, kind="Internal").ap()

        spill = {n: dram(f"spill_{n}", [2, 2, NH, HD, T], F16) for n in split}
        zero_dram = dram("zero_dram", [32, PAIRS * 2 * T], F16)
        o_dram = {k: dram(f"o_dram_{k}", [2, 4, 2, HD, 2, C, T]) for k in KINDS}
        r_dram = {k: dram(f"r_dram_{k}", [2, 4, 2, C * T]) for k in KINDS}
        rows_a_dram, rows_b_dram = dram("rows_a_dram", [NB, 2, D]), dram("rows_b_dram", [NB, 2, D])
        bc_dram = dram("bc_dram", [1, D])

        ready = {n: sem(f"ready_{n}") for n in DENSE}
        taken = {n: sem(f"taken_{n}") for n in DENSE}
        max_ready = {k: sem(f"max_ready_{k}") for k in KINDS}
        max_taken = {k: sem(f"max_taken_{k}") for k in KINDS}
        exp_ready = {k: sem(f"exp_ready_{k}") for k in KINDS}
        exp_taken = {k: sem(f"exp_taken_{k}") for k in KINDS}
        av_done = {k: sem(f"av_done_{k}") for k in KINDS}
        mh_step = {k: sem(f"mh_step_{k}") for k in KINDS}
        o_copied = {k: sem(f"o_copied_{k}") for k in KINDS}
        o_recip = {k: sem(f"o_recip_{k}") for k in KINDS}
        o_mult = {k: sem(f"o_mult_{k}") for k in KINDS}
        ot_hi, ot_lo = ({k: sem(f"{n}_{k}") for k in KINDS} for n in ("ot_hi", "ot_lo"))
        stats_done, mv_done = ({k: sem(f"{n}_{k}") for k in LN} for n in ("stats", "mv"))
        norm_step = {k: sem(f"norm_step_{k}") for k in LN}
        hi_done = {n: sem(f"hi_{n}") for n in ("t1", "t2", "tc", "t3", "q", "k", "qc", "kc")}
        g_hi, g_lo = sem("g_hi"), sem("g_lo")
        cols_a_set, cols_b_set = sem("cols_a_set"), sem("cols_b_set")
        xr_done, xc_done, xm_done = sem("xr_done"), sem("xc_done"), sem("xm_done")
        x2_done, y_done = sem("x2_done"), sem("y_done")
        x_in, c_in, stored = sems("x_in"), sems("c_in"), sems("stored")
        rows_a_in, rows_b_in = sems("rows_a_in"), sems("rows_b_in")
        spilled = {n: sems(f"spilled_{n}") for n in split}
        stacked = {n: sems(f"stacked_{n}") for n in split}
        mrow_in = {k: sems(f"mrow_{k}") for k in KINDS}
        o_out, o_n_in, o_d_in, r_out, o_rb_in = (
            {k: sems(f"{n}_{k}") for k in KINDS} for n in ("o_out", "o_n_in", "o_d_in", "r_out", "o_rb_in"))
        passed = sem("passed")
        setup_in, w_in = sem("setup_in"), [sem(f"w_in_{i}") for i in range(4)]
        w_hi_done, w_lo_done, late_in = sem("w_hi_done"), sem("w_lo_done"), sem("late_in")
        zeroed, ident_zero, ident_made, consts = sem("zeroed"), sem("ident_zero"), sem("ident_made"), sem("consts")
        pe_set, dve_set, act_set, sp_set = sem("pe_set"), sem("dve_set"), sem("act_set"), sem("sp_set")

        QKV_OF = {"q": "self", "k": "self", "qc": "cross", "kc": "cross"}

        def dmas(b, n):
            return (b.pair + 1) * (16 * n)

        def wait_dmas_before(eng, pair_of_sems, b, n):
            if isinstance(b.n, int) and b.n == 0:
                return
            eng.wait_ge(pair_of_sems[1 - b.u], dmas(Batch(b.pair, b.u - 1), n))

        def wait_count(eng, s, value):
            if not isinstance(value, int) or value > 0:
                eng.wait_ge(s, value)

        def apart(eng):
            eng.sem_inc(passed, 1)

        def flat(t):
            return t[:].rearrange("p a b -> p (a b)")

        stage = {"qkv": flat(probs)[:, 0:C * 3 * D], "proj": flat(probs)[:, C * 3 * D:C * 4 * D], "mlp1": flat(G),
                 "kvc": flat(o_sb["self"]), "qc": flat(o_n["self"]), "cproj": flat(o_n["cross"]),
                 "mlp2": g_split[:].rearrange("p s f t -> p (s f t)").bitcast(F32)}
        staged = {n: t.rearrange("p (k n) -> p k n", k=w_shapes[n][0]) for n, t in stage.items()}
        W_ORDER = ("qkv", "mlp1", "kvc", "proj", "qc", "cproj", "mlp2")
        EARLY_W = W_ORDER[:-1]
        w_wait = {"qkv": (0, 16), "mlp1": (1, 16), "kvc": (2, 64), "proj": (2, 64), "qc": (2, 64), "cproj": (2, 64),
                  "mlp2": (3, 16)}

        W_SPLITS = {"qkv": [(slice(0, D), HD ** -0.5), (slice(D, 3 * D), 1.0)], "qc": [(slice(0, D), HD ** -0.5)]}

        def w_parts(name):
            return W_SPLITS.get(name, [(slice(0, w_shapes[name][1]), 1.0)])

        q_flat = q_stack["self"][:].rearrange("p u a b -> p (u a b)")
        room = q_stack["cross"][:].rearrange("p u a b -> p (u a b)").bitcast(F32)
        MOD = room[0:NB, 0:6 * D]
        b_mod_rows = room[0:NB, 6 * D:12 * D]
        room2 = k_stack["cross"][:].rearrange("p u a b -> p (u a b)").bitcast(F32)
        cnd, cexp, cden, crec = (room2[0:NB, i * D:(i + 1) * D] for i in range(4))
        csil, v_bias = room2[0:NB, 4 * D:5 * D], room2[0:NB, 5 * D:6 * D]
        wm = V["self"][:].rearrange("p u t h d -> p (u t h d)")
        wm2 = V["cross"][:].rearrange("p u t h d -> p (u t h d)")
        room3, room4 = (t[:].rearrange("p u a b -> p (u a b)") for t in (X2, XC))
        b_rows = {n: room3[0:NB, i * D:(i + 1) * D] for i, n in enumerate(("v", "proj", "cproj", "mlp2"))}
        gb_a, gb_m, bc_row = (room4[0:NB, i * D:(i + 1) * D] for i in range(3))
        cT = sb("cT", [P, C, NB])
        shT = sb("shT", [P, 2, 4, NB], F16)
        vbT = sb("vbT", [P, 2, C, NB], F16)
        vcT = sb("vcT", [P, 2, C, NB], F16)
        vc_wide = sb("vc_wide", [P, C, NB])
        b_qk_col = sb("b_qk_col", [P, 2 * C])
        b_m1_col = sb("b_m1_col", [P, FC])
        b_kvc_col = sb("b_kvc_col", [P, 2 * C])

        def three(eng, dst, a_hi, a_lo, b_hi, b_lo, first=True, last=True):
            eng.matmul(dst, a_hi, b_hi, start=first, stop=False)
            eng.matmul(dst, a_hi, b_lo, start=False, stop=False)
            return eng.matmul(dst, a_lo, b_hi, start=False, stop=last)

        stack.enter_context(nc.allow_non_contiguous_dma(reason="bias columns, stacked heads"))
        block = stack.enter_context(nc.Block())

        @block.sync
        def _(sp):
            nc.sync.dma_start(cnd, cond).then_inc(setup_in, 16)
            wm_dram = W_mod.rearrange("(c p) n -> p c n", p=P)
            nc.sync.dma_start(wm[:, 0:6 * D], wm_dram[:, 0]).then_inc(setup_in, 16)
            nc.sync.dma_start(wm2[:, 0:6 * D], wm_dram[:, 1]).then_inc(setup_in, 16)
            nc.sync.dma_start(b_mod_rows, bass.AP(tensor=b_mod.tensor, offset=0, ap=[[0, NB], [1, 6 * D]])
                              ).then_inc(setup_in, 16)
            nc.sync.dma_start(b_qk_col[:], b_qkv.rearrange("(c p) -> p c", p=P)[:, 0:2 * C]).then_inc(setup_in, 16)

            def load_weight(name):
                nc.sync.dma_start(staged[name], w_dram[name].rearrange("(k p) n -> p k n", p=P)
                                  ).then_inc(w_in[w_wait[name][0]], 16)

            for name in W_ORDER[:4]:
                load_weight(name)
            sp.wait_ge(zeroed, 1)
            nc.sync.dma_start(zero_dram, q_flat[0:32, 0:PAIRS * 2 * T]).then_inc(sp_set, 16)
            for name in W_ORDER[4:]:
                load_weight(name)
            for name, src, start in (("v", b_qkv, 2 * D), ("proj", b_proj, 0), ("cproj", b_cproj, 0), ("mlp2", b_mlp2, 0)):
                nc.sync.dma_start(b_rows[name], bass.AP(tensor=src.tensor, offset=start, ap=[[0, NB], [1, D]])
                                  ).then_inc(late_in, 16)
            nc.sync.dma_start(b_m1_col[:], b_mlp1.rearrange("(c p) -> p c", p=P)).then_inc(late_in, 16)
            nc.sync.dma_start(cols_c[:, 0:C], b_qc.rearrange("(c p) -> p c", p=P)).then_inc(late_in, 16)
            nc.sync.dma_start(b_kvc_col[:], b_kvc.rearrange("(c p) -> p c", p=P)).then_inc(late_in, 16)
            sp.wait_ge(sp_set, 16)

            def late_setup():
                sp.wait_ge(dve_set, 12)
                nc.sync.dma_start(rows_a_dram[:, 0], MOD[:, 2 * D:3 * D]).then_inc(sp_set, 16)
                nc.sync.dma_start(rows_b_dram[:, 0], MOD[:, 5 * D:6 * D]).then_inc(sp_set, 16)
                nc.sync.dma_start(rows_a_dram[:, 1], gb_a).then_inc(sp_set, 16)
                nc.sync.dma_start(rows_b_dram[:, 1], gb_m).then_inc(sp_set, 16)
                nc.sync.dma_start(bc_dram, bc_row[0:1]).then_inc(sp_set, 16)
                sp.wait_ge(sp_set, 16 * 6)
                nc.sync.dma_start(bc_rows[:], bass.AP(tensor=bc_dram.tensor, offset=0, ap=[[0, P], [1, D]])).then_inc(sp_set, 16)

            def sp_wait(s, value):
                if not isinstance(value, int) or value > 0:
                    sp.wait_ge(s, value)
                    apart(sp)

            def load_x(b):
                sp_wait(xr_done, b.n - 1)
                sp_wait(norm_step["1"], (b.n - 1) * 3)
                nc.sync.dma_start(X[:, b.u], x[bass.ds(b.n, 1)].rearrange("a (t p) d -> p (a t) d", p=P)
                                  ).then_inc(x_in[b.u], 16)

            def load_c(b):
                sp_wait(norm_step["c"], b.n * 3)
                nc.sync.dma_start(Ctx[:], ctx_in[bass.ds(b.n, 1)].rearrange("a (t p) d -> p (a t) d", p=P)
                                  ).then_inc(c_in[b.u], 16)

            def load_rows(b, dst, src, s):
                row = src[bass.ds(b.n, 1)].rearrange("a r d -> a (r d)")
                nc.sync.dma_start(dst[:].rearrange("p r d -> p (r d)"), row.to_broadcast([P, 2 * D])
                                  ).then_inc(s[b.u], 16)

            def do_spill(b, n):
                sp_wait(taken[n], b.n + 1)
                nc.sync.dma_start(spill[n][b.u].rearrange("s (c h) d t -> (h d) s c t", c=C), split[n][:]
                                  ).then_inc(spilled[n][b.u], 16)

            def do_stack(b, n):
                kind = QKV_OF[n]
                if kind == "cross" and isinstance(b.n, int) and b.n == 0:
                    sp.wait_ge(consts, 3)
                sp_wait(spilled[n][b.u], dmas(b, 1))
                sp_wait(exp_ready[kind], (b.n - 1) * TILES)
                for part in range(3):
                    rows = slice(32 * part, 32 * part + 32)
                    if n[0] == "k":
                        src = spill[n][b.u, (1, 1, 0)[part]].rearrange("(p a) d t -> (a d) p t", a=2)
                        nc.sync.dma_start(k_stack[kind][rows, b.u], src).then_inc(stacked[n][b.u], 16)
                        continue
                    for ab in range(2):
                        src = spill[n][b.u, (0, 1, 1)[part]].rearrange("(p a) d t -> a d p t", a=2)[ab]
                        nc.sync.dma_start(q_stack[kind][32 * part + HD * ab:32 * part + HD * ab + HD, b.u, :, ab * T:(ab + 1) * T],
                                          src).then_inc(stacked[n][b.u], 16)
                if n[0] == "q":
                    nc.sync.dma_start(q_stack[kind][96:128, b.u].rearrange("p r t -> p (r t)"), zero_dram
                                      ).then_inc(stacked[n][b.u], 16)

            def mrow(b, kind):
                sp_wait(taken[f"m_{kind}"], b.n + 1)
                for ab in range(2):
                    nc.sync.dma_start(q_stack[kind][96 + 16 * ab:98 + 16 * ab, b.u, :, ab * T:(ab + 1) * T],
                                      mt[kind][16 * ab:16 * ab + 16]).then_inc(mrow_in[kind][b.u], 16)

            def o_store(b, kind, i):
                sp_wait(o_copied[kind], b.n * 4 + 2 * i + 2)
                nc.sync.dma_start(o_dram[kind][b.u].rearrange("j n d g c q -> (j n d) g c q")[:, :, i],
                                  o_sb[kind][:, i].rearrange("p (g q) -> p g q", g=2)).then_inc(o_out[kind][b.u], 16)

            def o_gather(b, kind):
                sp_wait(o_out[kind][b.u], dmas(b, 2))
                den = o_dram[kind][b.u][:, 1, 0].rearrange("j g c q -> j (g c q)").rearrange("j (a e) -> j a e", e=32)
                sp_wait(o_recip[kind], b.n)
                nc.sync.dma_start(o_d[kind][:], den).then_inc(o_d_in[kind][b.u], 16)
                sp_wait(ot_lo[kind], b.n)
                for gg in range(2):
                    num = o_dram[kind][b.u][:, 0].rearrange("j d g c q -> g j d (c q)")[gg]
                    nc.sync.dma_start(o_n[kind][64 * gg:64 * gg + 64].rearrange("p c q -> p (c q)"), num).then_inc(o_n_in[kind][b.u], 16)

            def r_store(b, kind):
                sp_wait(o_recip[kind], b.n + 1)
                flat = r_dram[kind][b.u].rearrange("j g (a e) -> (j g a) e", e=32)
                nc.sync.dma_start(flat, o_r[kind][:]).then_inc(r_out[kind][b.u], 16)

            def r_fetch(b, kind):
                sp_wait(r_out[kind][b.u], dmas(b, 1))
                sp_wait(o_mult[kind], b.n)
                for gg in range(2):
                    src = r_dram[kind][b.u, :, gg]
                    (j_step, j_n), (e_step, e_n) = [tuple(v) for v in src.ap]
                    nc.sync.dma_start(o_rb[kind][64 * gg:64 * gg + 64].rearrange("p c q -> p (c q)"),
                                      bass.AP(tensor=src.tensor, offset=src.offset,
                                              ap=[[j_step, j_n], [0, HD], [e_step, e_n]])).then_inc(o_rb_in[kind][b.u], 16)

            def store(b):
                sp_wait(y_done, b.n + 1)
                nc.sync.dma_start(out[bass.ds(b.n, 1)].rearrange("a (t p) d -> p (a t) d", p=P), Y[:]
                                  ).then_inc(stored[b.u], 16)

            def body(it):
                def at(half, s, due):
                    if (b := due("load_x")):
                        load_x(b)
                    if (b := due("rows_a")):
                        sp_wait(taken["proj"], b.n)
                        load_rows(b, rows_a, rows_a_dram, rows_a_in)
                    if (b := due("rows_b")):
                        sp_wait(taken["mlp2"], b.n)
                        load_rows(b, rows_b, rows_b_dram, rows_b_in)
                    if (b := due("load_c")):
                        load_c(b)
                    for kind in KINDS:
                        if (b := due(f"m_copy_{kind}")):
                            mrow(b, kind)
                    for n in split:
                        if (b := due(f"spill_{n}")):
                            do_spill(b, n)
                        if (b := due(f"stack_{n}")):
                            do_stack(b, n)
                    for kind in KINDS:
                        for i in range(2):
                            if (b := due(f"o_store{i}_{kind}")):
                                o_store(b, kind, i)
                        if (b := due(f"o_gather_{kind}")):
                            o_gather(b, kind)
                        if (b := due(f"r_out_{kind}")):
                            r_store(b, kind)
                        if (b := due(f"r_back_{kind}")):
                            r_fetch(b, kind)
                    if (b := due("store")):
                        store(b)
                slots(it, at)

            iterations(sp, body, late_setup)
            for u in range(2):
                sp.wait_ge(stored[u], 16 * NB // 2)

        @block.tensor
        def _(pe):
            pe.wait_ge(ident_made, 1)
            pe.wait_ge(dve_set, 1)
            for c in range(C):
                mm = pe.transpose(dense_ps[:, 0, c * NB:(c + 1) * NB], csil[:, c * P:(c + 1) * P], ident[0:NB, 0:NB])
            mm.then_inc(pe_set, 1)
            pe.wait_ge(dve_set, 2)
            for i in range(3):
                dst = (max_ps, max_ps, exp_ps)[i][0:NB, i % 2]
                for c in range(C):
                    mm = pe.matmul(dst, cT[:, c], (wm, wm2)[c][:, i * 512:(i + 1) * 512], start=c == 0, stop=c == C - 1)
            mm.then_inc(pe_set, 1)
            pe.wait_ge(dve_set, 3)
            for i, part in enumerate((0, 1, 3, 4)):
                for c in range(C):
                    mm = pe.transpose(dense_ps[:, 1, (2 * i + c) * NB:(2 * i + c + 1) * NB],
                                      MOD[:, part * D + c * P:part * D + (c + 1) * P], ident[0:NB, 0:NB])
            mm.then_inc(pe_set, 1)
            pe.wait_ge(dve_set, 5)
            pe.wait_ge(w_lo_done, 1)
            sh = lambda part, lo, c: shT[:, lo, 2 * part + c]
            for m in range(2 * C):
                for c in range(C):
                    w = slice(m * P, (m + 1) * P)
                    mm = three(pe, dense_ps[:, 0, m * NB:(m + 1) * NB], w_hi["qkv"][:, c, w], w_lo["qkv"][:, c, w],
                               sh(0, 0, c), sh(0, 1, c), c == 0, c == C - 1)
            mm.then_inc(pe_set, 1)
            pe.wait_ge(dve_set, 6)

            def late_setup():
                pe.wait_ge(w_lo_done, len(EARLY_W))
                for m in range(FC):
                    for c in range(C):
                        w = slice(m * P, (m + 1) * P)
                        three(pe, max_ps[:, 0, m * NB:(m + 1) * NB], w_hi["mlp1"][:, c, w], w_lo["mlp1"][:, c, w],
                              sh(1, 0, c), sh(1, 1, c), c == 0, c == C - 1)
                for c in range(C):
                    w = slice(2 * D, 3 * D)
                    mm = three(pe, max_ps[0:NB, 1, 0:D], sh(0, 0, c), sh(0, 1, c), w_hi["qkv"][:, c, w],
                               w_lo["qkv"][:, c, w], c == 0, c == C - 1)
                mm.then_inc(pe_set, 1)
                pe.wait_ge(dve_set, 8)
                for c in range(C):
                    pe.transpose(o_ps[:, 0, c * NB:(c + 1) * NB], v_bias[:, c * P:(c + 1) * P], ident[0:NB, 0:NB]
                                 ).then_inc(pe_set, 1)
                for c in range(C):
                    mm = three(pe, exp_ps[0:NB, 0, 0:D], vcT[:, 0, c], vcT[:, 1, c], w_hi["cproj"][:, c],
                               w_lo["cproj"][:, c], c == 0, c == C - 1)
                mm.then_inc(pe_set, 1)
                pe.wait_ge(dve_set, 10)
                for c in range(C):
                    mm = three(pe, exp_ps[0:NB, 1, 0:D], vbT[:, 0, c], vbT[:, 1, c], w_hi["proj"][:, c],
                               w_lo["proj"][:, c], c == 0, c == C - 1)
                mm.then_inc(pe_set, 1)
                pe.wait_ge(dve_set, 12)

            def last_setup():
                pe.wait_ge(consts, 2)

            def tenant(it, unit):
                mates = [n for n in DENSE if DENSE[n] == DENSE[unit]]
                if (prev := previous(it, mates, dense_lags, unit)):
                    pe.wait_ge(taken[prev[0]], prev[1].n + 1)
                return dense_ps[:, DENSE[unit]]

            def turn(it, b, unit, k):
                pe.wait_ge(norm_step[k], b.n * 3 + 3)
                ps = tenant(it, unit)
                for c in range(C):
                    for t in range(2):
                        mm = pe.transpose(ps[:, c * T + t * P:c * T + (t + 1) * P], xn[k][:, t, c * P:(c + 1) * P], ident[:])
                mm.then_inc(ready[unit], 1)

            def features_out(it, unit, src, name, col):
                ps = tenant(it, unit)
                for m in range(2):
                    for c in range(C):
                        w = slice(col + m * P, col + (m + 1) * P)
                        mm = three(pe, ps[:, m * T:(m + 1) * T], w_hi[name][:, c, w], w_lo[name][:, c, w],
                                   src[:, 0, c], src[:, 1, c], c == 0, c == C - 1)
                mm.then_inc(ready[unit], 1)

            def tokens_out(it, unit, src, name, col):
                ps = tenant(it, unit)
                for t in range(2):
                    tok = slice(t * P, (t + 1) * P)
                    for c in range(C):
                        mm = three(pe, ps[:, t * D:(t + 1) * D], src[:, 0, c, tok], src[:, 1, c, tok],
                                   w_hi[name][:, c, col:col + D], w_lo[name][:, c, col:col + D], c == 0, c == C - 1)
                mm.then_inc(ready[unit], 1)

            def turn_maxima(it, b, kind):
                pe.wait_ge(mh_step[kind], b.n * 2 + 2)
                ps = tenant(it, f"m_{kind}")
                for qt in range(2):
                    mm = pe.transpose(ps[0:32, 0:P].bitcast(F16)[:, qt * P:(qt + 1) * P],
                                      mh[kind][:, qt].rearrange("p a s r -> p (a s r)"), ident16[:])
                mm.then_inc(ready[f"m_{kind}"], 1)

            def mlp2_part(it, b, part):
                t, half = part // 2, part % 2
                if part == 0:
                    pe.wait_ge(g_lo, b.n * 4 + 4)
                    tenant(it, "mlp2")
                ps = dense_ps[:, DENSE["mlp2"]]
                tok = slice(t * P, (t + 1) * P)
                for f in range(half * FC // 2, (half + 1) * FC // 2):
                    mm = three(pe, ps[:, t * D:(t + 1) * D], g_split[:, 0, f, tok], g_split[:, 1, f, tok],
                               w_hi["mlp2"][:, f], w_lo["mlp2"][:, f], f == 0, f == FC - 1)
                if part == 3:
                    mm.then_inc(ready["mlp2"], 1)

            def maxima(it, kind, b, t):
                p, qt = t // 2, t % 2
                if t == 0:
                    for n in (("q", "k") if kind == "self" else ("qc", "kc")):
                        pe.wait_ge(stacked[n][b.u], dmas(b, 7 if n[0] == "q" else 3))
                if t >= 2:
                    pe.wait_ge(max_taken[kind], b.n * TILES + t - 1)
                elif (prev := previous(it, max_order, MAX_LAG, kind)):
                    pe.wait_ge(max_taken[prev[0]], prev[1].n * TILES + TILES - 1 + t)
                for ab in range(2):
                    mm = pe.matmul(max_ps[:, t % 2, ab * T:(ab + 1) * T],
                                   q_stack[kind][:, b.u, p, ab * T + qt * P:ab * T + (qt + 1) * P],
                                   k_stack[kind][:, b.u, p], start=True, stop=True)
                mm.then_inc(max_ready[kind], 1)

            def exps(it, kind, b, t):
                p, kt = t // 2, t % 2
                if t == 0:
                    pe.wait_ge(mrow_in[kind][b.u], dmas(b, 2))
                if t >= 2:
                    pe.wait_ge(exp_taken[kind], b.n * TILES + t - 1)
                elif (prev := previous(it, exp_order, EXP_LAG, kind)):
                    pe.wait_ge(exp_taken[prev[0]], prev[1].n * TILES + TILES - 1 + t)
                pe.matmul(exp_ps[:, t % 2], k_stack[kind][:, b.u, p, kt * P:(kt + 1) * P], q_stack[kind][:, b.u, p],
                          start=True, stop=True).then_inc(exp_ready[kind], 1)

            def values(it, kind, b, g):
                pe.wait_ge(exp_taken[kind], b.n * TILES + 4 * g + 4)
                if g == 0:
                    pe.wait_ge(taken["v" if kind == "self" else "vc"], b.n + 1)
                if g >= 2:
                    pe.wait_ge(o_copied[kind], b.n * 4 + g - 1)
                elif (prev := previous(it, exp_order, EXP_LAG, kind)):
                    pe.wait_ge(o_copied[prev[0]], prev[1].n * 4 + g + 3)
                for kt in range(2):
                    for j in range(4):
                        tile = 4 * g + 2 * (j // 2) + kt
                        mm = pe.matmul(o_ps[32 * j:32 * j + 32, 0, (g % 2) * T:(g % 2 + 1) * T],
                                       V[kind][:, b.u, kt, 4 * g + j], probs[:, tile % 8, (j % 2) * T:(j % 2 + 1) * T],
                                       start=kt == 0, stop=kt == 1, tile_position=(0, 32 * j),
                                       skip_group_check=True)
                mm.then_inc(av_done[kind], 1)

            def body(it):
                def at(half, s, due):
                    if (m := max_tile(it, half, s)):
                        maxima(it, *m)
                    if (e := exp_tile(it, half, s)):
                        exps(it if (half, s >= EXP_START) != (0, False) else it.before(), *e)
                    if (v := av_group(it, half, s)):
                        values(it if not (half == 0 and s < EXP_START + AV_AFTER) else it.before(), *v)
                    for kind in KINDS:
                        if (b := due(f"m_{kind}")):
                            turn_maxima(it, b, kind)
                    if (b := due("qc")):
                        pe.wait_ge(taken["t2"], b.n + 1)
                        features_out(it, "qc", xt["2"], "qc", 0)
                    if (b := due("cproj")):
                        pe.wait_ge(ot_lo["cross"], b.n + 1)
                        tokens_out(it, "cproj", ot["cross"], "cproj", 0)
                    if (b := due("tc")):
                        turn(it, b, "tc", "c")
                    if (b := due("kc")):
                        pe.wait_ge(taken["tc"], b.n + 1)
                        features_out(it, "kc", xt["c"], "kvc", 0)
                    if (b := due("t3")):
                        turn(it, b, "t3", "3")
                    for i in range(4):
                        if (b := due(f"mlp1_{i}")):
                            pe.wait_ge(taken["t3"], b.n + 1)
                            features_out(it, f"mlp1_{i}", xt["3"], "mlp1", 2 * i * P)
                    if (b := due("vc")):
                        tokens_out(it, "vc", xt["c"], "kvc", D)
                    if (b := due("t1")):
                        turn(it, b, "t1", "1")
                    if (b := due("proj")):
                        pe.wait_ge(ot_lo["self"], b.n + 1)
                        tokens_out(it, "proj", ot["self"], "proj", 0)
                    for i in range(4):
                        if (b := due(f"mlp2_{i}")):
                            mlp2_part(it, b, i)
                    if (b := due("q")):
                        pe.wait_ge(taken["t1"], b.n + 1)
                        features_out(it, "q", xt["1"], "qkv", 0)
                    if (b := due("k")):
                        features_out(it, "k", xt["1"], "qkv", D)
                    if (b := due("v")):
                        tokens_out(it, "v", xt["1"], "qkv", 2 * D)
                    if (b := due("t2")):
                        turn(it, b, "t2", "2")
                slots(it, at)

            iterations(pe, body, late_setup, last_setup)

        @block.scalar
        def _(act):
            def split_weight(name):
                s, value = w_wait[name]
                act.wait_ge(w_in[s], value)
                for cols, scale in w_parts(name):
                    last = nc.scalar.activation(w_hi[name][:, :, cols], staged[name][:, :, cols], ACT.Copy, scale=scale)
                last.then_inc(w_hi_done, 1)

            act.wait_ge(setup_in, 16 * 5)
            nc.scalar.activation(cexp, cnd, ACT.Exp, scale=-1.0).then_inc(act_set, 1)
            for name in EARLY_W:
                split_weight(name)

            def late_setup():
                split_weight("mlp2")

            def turn_hi(b, unit, k, scales):
                act.wait_ge(ready[unit], b.n + 1)
                reader = {"1": "v", "2": "qc", "c": "vc", "3": "mlp1_3"}[k]
                wait_count(act, ready[reader], b.n)
                if scales is None:
                    last = nc.scalar.activation(xt[k][:, 0].rearrange("p c t -> p (c t)"), bank(unit), ACT.Copy)
                else:
                    for c in range(C):
                        last = nc.scalar.activation(xt[k][:, 0, c], bank(unit)[:, c * T:(c + 1) * T], ACT.Copy,
                                                    scale=scales[c])
                last.then_inc(hi_done[unit], 1)

            def bank(unit):
                return dense_ps[:, DENSE[unit]]

            def project_hi(b, n, biases):
                act.wait_ge(ready[n], b.n + 1)
                wait_dmas_before(act, spilled[n], b, 1)
                for c in range(C):
                    last = nc.scalar.activation(split[n][:, 1, c], bank(n)[:, c * T:(c + 1) * T], ACT.Identity,
                                                bias=biases[c])
                last.then_inc(hi_done[n], 1)

            def keep_values(b, unit, kind):
                act.wait_ge(ready[unit], b.n + 1)
                wait_count(act, av_done[kind], (b.n - 1) * 4)
                nc.scalar.activation(V[kind][:, b.u].rearrange("p t h e -> p (t h) e")[:, :, 0:HD],
                                     bank(unit).rearrange("p (h e) -> p h e", e=HD), ACT.Copy).then_inc(taken[unit], 1)

            act.wait_ge(consts, 1)

            def body(it):
                def at(half, s, due):
                    if (e := exp_tile(it, half, s)):
                        kind, b, t = e
                        act.wait_ge(exp_ready[kind], b.n * TILES + t + 1)
                        if t >= 8:
                            act.wait_ge(av_done[kind], b.n * 4 + t // 4 - 1)
                        else:
                            src = it if (half, s >= EXP_START) != (0, False) else it.before()
                            if (prev := previous(src, exp_order, EXP_LAG, kind)):
                                act.wait_ge(av_done[prev[0]], prev[1].n * 4 + t // 4 + 3)
                        nc.scalar.activation(probs[:, t % 8], exp_ps[:, t % 2], ACT.Exp).then_inc(exp_taken[kind], 1)
                    if (v := av_group(it, half, s)):
                        kind, b, g = v
                        act.wait_ge(av_done[kind], b.n * 4 + g + 1)
                        wait_dmas_before(act, o_out[kind], b, 2)
                        cols = slice((g % 2) * T, (g % 2 + 1) * T)
                        nc.scalar.activation(o_sb[kind][:, g // 2, cols], o_ps[:, 0, cols], ACT.Copy).then_inc(o_copied[kind], 1)
                    if (b := due("tc_hi")):
                        turn_hi(b, "tc", "c", None)
                    if (b := due("kc_hi")):
                        project_hi(b, "kc", [cols_c[:, C + c:C + c + 1] for c in range(C)])
                    if (b := due("vc_hi")):
                        keep_values(b, "vc", "cross")
                    if (b := due("t3_hi")):
                        act.wait_ge(cols_b_set, b.n + 1)
                        turn_hi(b, "t3", "3", [cols_b[:, c:c + 1] for c in range(C)])
                    if (b := due("gelu")):
                        wait_count(act, g_lo, b.n * 4)
                        for i in range(4):
                            act.wait_ge(ready[f"mlp1_{i}"], b.n + 1)
                            for m in range(2):
                                f = 2 * i + m
                                last = nc.scalar.activation(G[:, f], bank(f"mlp1_{i}")[:, m * T:(m + 1) * T],
                                                            ACT.Gelu_apprx_tanh, bias=cols_b[:, C + f:C + f + 1])
                            last.then_inc(taken[f"mlp1_{i}"], 1)
                    if (b := due("t1_hi")):
                        act.wait_ge(cols_a_set, b.n + 1)
                        turn_hi(b, "t1", "1", [cols_a[:, b.u, 4 + c:5 + c] for c in range(C)])
                    if (b := due("q_hi")):
                        project_hi(b, "q", [cols_a[:, b.u, c:c + 1] for c in range(C)])
                    if (b := due("k_hi")):
                        project_hi(b, "k", [cols_a[:, b.u, C + c:C + c + 1] for c in range(C)])
                    if (b := due("v_hi")):
                        keep_values(b, "v", "self")
                    if (b := due("t2_hi")):
                        turn_hi(b, "t2", "2", None)
                    if (b := due("qc_hi")):
                        project_hi(b, "qc", [cols_c[:, c:c + 1] for c in range(C)])
                slots(it, at)

            iterations(act, body, late_setup)

        @block.vector
        def _(dve):
            dve.wait_ge(act_set, 1)
            chain = sem("dve_chain")
            links = [0]

            def then(ins):
                links[0] += 1
                ins.then_inc(chain, 1)
                dve.wait_ge(chain, links[0])

            then(nc.vector.tensor_scalar_add(cden, cexp, 1.0))
            then(nc.vector.reciprocal(crec, cden))
            nc.vector.tensor_tensor(csil, cnd, crec, ALU.mult).then_inc(dve_set, 1)
            dve.wait_ge(pe_set, 1)
            nc.vector.tensor_copy(cT[:].rearrange("p c b -> p (c b)"), dense_ps[:, 0, 0:C * NB]).then_inc(dve_set, 1)

            def split_weight(name):
                dve.wait_ge(w_hi_done, W_ORDER.index(name) + 1)
                for cols, scale in w_parts(name):
                    last = nc.vector.scalar_tensor_tensor(out=w_lo[name][:, :, cols], in0=staged[name][:, :, cols], scalar=scale,
                                                          in1=w_hi[name][:, :, cols], op0=ALU.mult, op1=ALU.subtract)
                last.then_inc(w_lo_done, 1)

            for name in EARLY_W[:4]:
                split_weight(name)
            dve.wait_ge(pe_set, 2)
            for i in range(3):
                last = nc.vector.tensor_tensor(MOD[:, i * 512:(i + 1) * 512], (max_ps, max_ps, exp_ps)[i][0:NB, i % 2],
                                               b_mod_rows[:, i * 512:(i + 1) * 512], ALU.add)
            last.then_inc(dve_set, 1)
            dve.wait_ge(pe_set, 3)
            turned = dense_ps[:, 1, 0:8 * NB].rearrange("p (i c b) -> p i c b", i=4, c=C)
            for part, i in ((0, 0), (1, 2)):
                last = nc.vector.tensor_copy(shT[:, 0, 2 * part:2 * part + 2], turned[:, i])
            last.then_inc(dve_set, 1)
            dve.wait_ge(dve_set, 4)
            for part, i in ((0, 0), (1, 2)):
                last = nc.vector.tensor_tensor(shT[:, 1, 2 * part:2 * part + 2], turned[:, i],
                                               shT[:, 0, 2 * part:2 * part + 2], ALU.subtract)
            last.then_inc(dve_set, 1)
            for i, dst in ((1, cols_a_all[:, :, 4:6]), (3, cols_b_all[:, :, 0:C])):
                nc.vector.tensor_scalar_add(dst.rearrange("p b c -> p c b"), turned[:, i], 1.0)
            then(nc.vector.tensor_scalar_mul(b_qk_col[:, 0:C], b_qk_col[:, 0:C], HD ** -0.5))
            dve.wait_ge(pe_set, 4)
            for m in range(2 * C):
                last = nc.vector.tensor_scalar_add(cols_a_all[:, :, m], dense_ps[:, 0, m * NB:(m + 1) * NB], b_qk_col[:, m:m + 1])
            last.then_inc(dve_set, 1)
            dve.wait_ge(dve_set, 6)

            def late_setup():
                for name in EARLY_W[4:]:
                    split_weight(name)
                dve.wait_ge(late_in, 16 * 7)
                nc.vector.tensor_scalar_mul(cols_c[:, 0:C], cols_c[:, 0:C], HD ** -0.5)
                nc.vector.tensor_copy(cols_c[:, C:2 * C], b_kvc_col[:, 0:C])
                then(nc.vector.memset(vc_wide[:], 0.0))
                for c in range(C):
                    last = nc.vector.tensor_scalar_add(vc_wide[:, c], vc_wide[:, c], b_kvc_col[:, C + c:C + c + 1])
                then(last)
                then(nc.vector.tensor_copy(vcT[:, 0], vc_wide[:]))
                nc.vector.tensor_tensor(vcT[:, 1], vc_wide[:], vcT[:, 0], ALU.subtract).then_inc(dve_set, 1)
                dve.wait_ge(pe_set, 5)
                nc.vector.tensor_tensor(v_bias, max_ps[0:NB, 1, 0:D], b_rows["v"], ALU.add).then_inc(dve_set, 1)
                for m in range(FC):
                    nc.vector.tensor_scalar_add(cols_b_all[:, :, C + m], max_ps[:, 0, m * NB:(m + 1) * NB], b_m1_col[:, m:m + 1])
                dve.wait_ge(pe_set, 7)
                vb_ps = o_ps[:, 0, 0:C * NB].rearrange("p (c b) -> p c b", c=C)
                nc.vector.tensor_copy(vbT[:, 0], vb_ps).then_inc(dve_set, 1)
                dve.wait_ge(dve_set, 9)
                nc.vector.tensor_tensor(vbT[:, 1], vb_ps, vbT[:, 0], ALU.subtract).then_inc(dve_set, 1)
                dve.wait_ge(pe_set, 8)
                nc.vector.tensor_tensor(bc_row, exp_ps[0:NB, 0, 0:D], b_rows["cproj"], ALU.add)
                nc.vector.tensor_tensor(gb_m, MOD[:, 5 * D:6 * D], b_rows["mlp2"], ALU.mult).then_inc(dve_set, 1)
                dve.wait_ge(pe_set, 9)
                then(nc.vector.tensor_tensor(gb_a, exp_ps[0:NB, 1, 0:D], b_rows["proj"], ALU.add))
                nc.vector.tensor_tensor(gb_a, gb_a, MOD[:, 2 * D:3 * D], ALU.mult).then_inc(dve_set, 1)
                dve.wait_ge(dve_set, 12)

            def bank(unit):
                return dense_ps[:, DENSE[unit]]

            def statistics(b, k, src):
                for t in range(2):
                    last = nc.vector.bn_stats(stats[k][:, t], src[:, t])
                last.then_inc(stats_done[k], 1)
                dve.wait_ge(stats_done[k], b.n + 1)
                wait_count(dve, norm_step[k], b.n * 3)
                apart(dve)
                for t in range(2):
                    last = nc.vector.bn_aggr(mv[k][:, t], stats[k][:, t])
                last.then_inc(mv_done[k], 1)

            def turn_lo(b, unit, k, scales):
                dve.wait_ge(hi_done[unit], b.n + 1)
                if scales is None:
                    last = nc.vector.tensor_tensor(xt[k][:, 1].rearrange("p c t -> p (c t)"), bank(unit),
                                                   xt[k][:, 0].rearrange("p c t -> p (c t)"), ALU.subtract)
                else:
                    for c in range(C):
                        last = nc.vector.scalar_tensor_tensor(out=xt[k][:, 1, c], in0=bank(unit)[:, c * T:(c + 1) * T],
                                                              scalar=scales[c], in1=xt[k][:, 0, c],
                                                              op0=ALU.mult, op1=ALU.subtract)
                last.then_inc(taken[unit], 1)

            def project_lo(b, n, biases):
                dve.wait_ge(hi_done[n], b.n + 1)
                for c in range(C):
                    last = nc.vector.scalar_tensor_tensor(out=split[n][:, 0, c], in0=bank(n)[:, c * T:(c + 1) * T],
                                                          scalar=biases[c], in1=split[n][:, 1, c],
                                                          op0=ALU.add, op1=ALU.subtract)
                last.then_inc(taken[n], 1)

            def split_maxima(b, kind):
                wait_count(dve, ready[f"m_{kind}"], b.n)
                dve.wait_ge(max_taken[kind], (b.n + 1) * TILES)
                view = mh[kind][:].rearrange("p q a s r -> p (q a) s r")
                top = mx[kind][:].rearrange("p q a r -> p (q a) r")
                nc.vector.tensor_scalar_mul(view[:, :, 0], top, -1.0 / SHIFT_UNIT).then_inc(mh_step[kind], 1)
                dve.wait_ge(mh_step[kind], b.n * 2 + 1)
                nc.vector.scalar_tensor_tensor(out=view[:, :, 1], in0=top, scalar=-1.0 / SHIFT_UNIT, in1=view[:, :, 0],
                                               op0=ALU.mult, op1=ALU.subtract).then_inc(mh_step[kind], 1)

            def body(it):
                def at(half, s, due):
                    for kind in KINDS:
                        if (b := due(f"split_{kind}")):
                            split_maxima(b, kind)
                        if (b := due(f"m_copy_{kind}")):
                            dve.wait_ge(ready[f"m_{kind}"], b.n + 1)
                            wait_dmas_before(dve, mrow_in[kind], b, 2)
                            nc.vector.tensor_copy(mt[kind][:], bank(f"m_{kind}")[0:32, 0:P].bitcast(F16)
                                                  ).then_inc(taken[f"m_{kind}"], 1)
                    if (m := max_tile(it, half, s)):
                        kind, b, t = m
                        dve.wait_ge(max_ready[kind], b.n * TILES + t + 1)
                        nc.vector.tensor_reduce(mx[kind][:, t % 2, :, t // 2],
                                                max_ps[:, t % 2].rearrange("p (a k) -> p a k", a=2), AX_X, ALU.max
                                                ).then_inc(max_taken[kind], 1)
                    if (b := due("cols_a")):
                        wait_count(dve, taken["k"], b.n - 1)
                        nc.vector.tensor_scalar_add(cols_a[:, b.u], cols_a_all[:, bass.ds(b.n, 1)].rearrange("p a c -> p (a c)"), 0.0
                                                    ).then_inc(cols_a_set, 1)
                    if (b := due("cols_b")):
                        wait_count(dve, taken["mlp1_3"], b.n)
                        nc.vector.tensor_scalar_add(cols_b[:], cols_b_all[:, bass.ds(b.n, 1)].rearrange("p a c -> p (a c)"), 0.0
                                                    ).then_inc(cols_b_set, 1)
                    if (b := due("ln1")):
                        dve.wait_ge(x_in[b.u], dmas(b, 1))
                        statistics(b, "1", X[:, b.u])
                    for kind in KINDS:
                        if (b := due(f"o_recip_{kind}")):
                            dve.wait_ge(o_d_in[kind][b.u], dmas(b, 1))
                            wait_dmas_before(dve, r_out[kind], b, 1)
                            nc.vector.reciprocal(o_r[kind][:], o_d[kind][:]).then_inc(o_recip[kind], 1)
                        if (b := due(f"o_hi_{kind}")):
                            dve.wait_ge(o_mult[kind], b.n + 1)
                            wait_count(dve, ready["proj" if kind == "self" else "cproj"], b.n)
                            nc.vector.tensor_copy(ot[kind][:, 0], o_n[kind][:]).then_inc(ot_hi[kind], 1)
                            dve.wait_ge(ot_hi[kind], b.n + 1)
                            nc.vector.tensor_tensor(ot[kind][:, 1], o_n[kind][:], ot[kind][:, 0], ALU.subtract
                                                    ).then_inc(ot_lo[kind], 1)
                    if (b := due("x3")):
                        dve.wait_ge(ready["cproj"], b.n + 1)
                        dve.wait_ge(xc_done, b.n + 1)
                        wait_count(dve, y_done, b.n)
                        nc.vector.tensor_tensor(X3[:].rearrange("p t d -> p (t d)"), bank("cproj"),
                                                XC[:, b.u].rearrange("p t d -> p (t d)"), ALU.add).then_inc(taken["cproj"], 1)
                    if (b := due("ln3")):
                        dve.wait_ge(taken["cproj"], b.n + 1)
                        statistics(b, "3", X3)
                    if (b := due("tc_lo")):
                        turn_lo(b, "tc", "c", None)
                    if (b := due("kc_lo")):
                        project_lo(b, "kc", [cols_c[:, C + c:C + c + 1] for c in range(C)])
                    if (b := due("t3_lo")):
                        turn_lo(b, "t3", "3", [cols_b[:, c:c + 1] for c in range(C)])
                    for i in range(4):
                        if (b := due(f"g_hi_{i}")):
                            if i == 0:
                                wait_count(dve, ready["mlp2"], b.n)
                            dve.wait_ge(taken[f"mlp1_{i}"], b.n + 1)
                            nc.vector.tensor_copy(g_split[:, 0, 2 * i:2 * i + 2], G[:, 2 * i:2 * i + 2]).then_inc(g_hi, 1)
                    if (b := due("x2")):
                        dve.wait_ge(ready["proj"], b.n + 1)
                        dve.wait_ge(rows_a_in[b.u], dmas(b, 1))
                        wait_count(dve, xc_done, b.n - 1)
                        nc.vector.tensor_tensor(X2[:, b.u], bank("proj").rearrange("p (t d) -> p t d", t=2),
                                                rows_a[:, 0:1].to_broadcast([P, 2, D]), ALU.mult).then_inc(taken["proj"], 1)
                        dve.wait_ge(taken["proj"], b.n + 1)
                        dve.wait_ge(xr_done, b.n + 1)
                        nc.vector.tensor_tensor(X2[:, b.u], X2[:, b.u], XR[:], ALU.add).then_inc(x2_done, 1)
                    if (b := due("ln2")):
                        dve.wait_ge(x2_done, b.n + 1)
                        statistics(b, "2", X2[:, b.u])
                    if (b := due("t1_lo")):
                        turn_lo(b, "t1", "1", [cols_a[:, b.u, 4 + c:5 + c] for c in range(C)])
                    if (b := due("q_lo")):
                        project_lo(b, "q", [cols_a[:, b.u, c:c + 1] for c in range(C)])
                    if (b := due("k_lo")):
                        project_lo(b, "k", [cols_a[:, b.u, C + c:C + c + 1] for c in range(C)])
                    if (b := due("y")):
                        dve.wait_ge(ready["mlp2"], b.n + 1)
                        dve.wait_ge(rows_b_in[b.u], dmas(b, 1))
                        wait_dmas_before(dve, stored, b, 1)
                        nc.vector.tensor_tensor(Y[:], bank("mlp2").rearrange("p (t d) -> p t d", t=2),
                                                rows_b[:, 0:1].to_broadcast([P, 2, D]), ALU.mult).then_inc(taken["mlp2"], 1)
                    if (b := due("t2_lo")):
                        turn_lo(b, "t2", "2", None)
                    if (b := due("qc_lo")):
                        project_lo(b, "qc", [cols_c[:, c:c + 1] for c in range(C)])
                    if (b := due("lnc")):
                        dve.wait_ge(c_in[b.u], dmas(b, 1))
                        statistics(b, "c", Ctx)
                slots(it, at)

            iterations(dve, body, late_setup)

        @block.gpsimd
        def _(pool):
            nc.gpsimd.memset(ident[:], 0.0).then_inc(ident_zero, 1)
            pool.wait_ge(ident_zero, 1)
            nc.gpsimd.affine_select(out=ident[:], in_=ident[:], compare_op=ALU.not_equal, fill=1.0, base=0,
                                    pattern=[[-1, P]], channel_multiplier=1).then_inc(ident_made, 1)
            pool.wait_ge(ident_made, 1)
            nc.gpsimd.tensor_copy(ident16[:], ident[:])
            nc.gpsimd.memset(neg_half[:], -0.5)
            nc.gpsimd.memset(q_stack["self"][:], 0.0).then_inc(zeroed, 1)
            nc.gpsimd.memset(k_stack["self"][:], SHIFT_UNIT)
            pool.wait_ge(pe_set, 2)
            for kind in KINDS:
                last = nc.gpsimd.memset(V[kind][:], 1.0)
            last.then_inc(consts, 1)

            def late_setup():
                pool.wait_ge(w_hi_done, len(W_ORDER))
                nc.gpsimd.tensor_tensor(w_lo["mlp2"][:], staged["mlp2"], w_hi["mlp2"][:], ALU.subtract).then_inc(consts, 1)

            def last_setup():
                pool.wait_ge(sp_set, 16 * 7)
                nc.gpsimd.memset(k_stack["cross"][:], SHIFT_UNIT)
                nc.gpsimd.memset(q_stack["cross"][:], 0.0).then_inc(consts, 1)

            def normalise(b, k, src):
                pool.wait_ge(mv_done[k], b.n + 1)
                apart(pool)
                nc.gpsimd.tensor_scalar(ve[k][:], mv[k][:, :, 1], LN_EPS, 1.0, ALU.add, ALU.mult).then_inc(norm_step[k], 1)
                nc.gpsimd.tensor_scalar(nm[k][:], mv[k][:, :, 0], -1.0, 0.0, ALU.mult, ALU.add)
                pool.wait_ge(norm_step[k], b.n * 3 + 1)
                nc.gpsimd.tensor_tensor(rs[k][:], ve[k][:], neg_half[:], ALU.pow).then_inc(norm_step[k], 1)
                pool.wait_ge(norm_step[k], b.n * 3 + 2)
                unit = {"1": "t1", "2": "t2", "c": "tc", "3": "t3"}[k]
                wait_count(pool, ready[unit], b.n)
                apart(pool)
                for t in range(2):
                    last = nc.gpsimd.tensor_scalar(xn[k][:, t], src[:, t], nm[k][:, t:t + 1], rs[k][:, t:t + 1],
                                                   ALU.add, ALU.mult)
                last.then_inc(norm_step[k], 1)

            def body(it):
                def at(half, s, due):
                    for kind in KINDS:
                        if (b := due(f"o_norm_{kind}")):
                            pool.wait_ge(o_n_in[kind][b.u], dmas(b, 2))
                            pool.wait_ge(o_rb_in[kind][b.u], dmas(b, 2))
                            nc.gpsimd.tensor_tensor(o_n[kind][:], o_n[kind][:], o_rb[kind][:], ALU.mult).then_inc(o_mult[kind], 1)
                    if (b := due("norm1")):
                        normalise(b, "1", X[:, b.u])
                    if (b := due("xr")):
                        pool.wait_ge(rows_a_in[b.u], dmas(b, 1))
                        wait_count(pool, x2_done, b.n)
                        nc.gpsimd.tensor_tensor(XR[:], X[:, b.u], rows_a[:, 1:2].to_broadcast([P, 2, D]), ALU.add
                                                ).then_inc(xr_done, 1)
                    if (b := due("xc")):
                        wait_count(pool, taken["cproj"], b.n - 1)
                        nc.gpsimd.tensor_tensor(XC[:, b.u], X2[:, b.u],
                                                bc_rows[:].rearrange("p (a d) -> p a d", a=1).to_broadcast([P, 2, D]), ALU.add
                                                ).then_inc(xc_done, 1)
                    if (b := due("xm")):
                        pool.wait_ge(taken["cproj"], b.n + 1)
                        pool.wait_ge(rows_b_in[b.u], dmas(b, 1))
                        pool.wait_ge(norm_step["3"], b.n * 3 + 3)
                        nc.gpsimd.tensor_tensor(X3[:], X3[:], rows_b[:, 1:2].to_broadcast([P, 2, D]), ALU.add
                                                ).then_inc(xm_done, 1)
                    if (b := due("norm3")):
                        normalise(b, "3", X3)
                    if (b := due("y_add")):
                        pool.wait_ge(taken["mlp2"], b.n + 1)
                        pool.wait_ge(xm_done, b.n + 1)
                        nc.gpsimd.tensor_tensor(Y[:], Y[:], X3[:], ALU.add).then_inc(y_done, 1)
                    for i in range(4):
                        if (b := due(f"g_lo_{i}")):
                            pool.wait_ge(g_hi, b.n * 4 + i + 1)
                            nc.gpsimd.tensor_tensor(g_split[:, 1, 2 * i:2 * i + 2], G[:, 2 * i:2 * i + 2],
                                                    g_split[:, 0, 2 * i:2 * i + 2], ALU.subtract).then_inc(g_lo, 1)
                    if (b := due("norm2")):
                        normalise(b, "2", X2[:, b.u])
                    if (b := due("normc")):
                        normalise(b, "c", Ctx)
                slots(it, at)

            iterations(pool, body, late_setup, last_setup)


_INS = ["x", "cond_1024", "ctx_1024"] + [f"L0_xcond_{n}" for n in (
    "W_mod", "b_mod", "W_qkv", "b_qkv", "W_proj", "b_proj", "W_qc", "b_qc", "W_kvc", "b_kvc",
    "W_cproj", "b_cproj", "W_mlp1", "b_mlp1", "W_mlp2", "b_mlp2")]


def kernel(**inputs):
    import numpy as np
    import concourse.bacc as bacc
    from concourse.bass_utils import run_bass_kernel_spmd

    nc = bacc.Bacc("TRN2", target_bir_lowering=False, num_devices=1)
    arrays, args = {}, []
    for name in _INS:
        a = np.ascontiguousarray(inputs[name])
        arrays[f"in_{name}"] = a
        args.append(nc.dram_tensor(f"in_{name}", a.shape, mybir.dt.from_np(a.dtype), kind="ExternalInput").ap())
    args.append(nc.dram_tensor("out_x", inputs["x"].shape, F32, kind="ExternalOutput").ap())
    block_kernel(nc, *args)
    return run_bass_kernel_spmd(nc, [arrays], core_ids=[0]).results[0]["out_x"]
```
